# Optimizing a Trainium2 kernel written in Bass

```python
import numpy as np
import jax
import jax.numpy as jnp

def _softmax(x, axis=-1):
    return jax.nn.softmax(x, axis=axis)

def _gelu(x):
    return jax.nn.gelu(x, approximate=True)

def _silu(x):
    return jax.nn.silu(x)

def _sigmoid(x):
    return jax.nn.sigmoid(x)

def _layernorm(x, axis=-1, eps=1e-05):
    m = jnp.mean(x, axis=axis, keepdims=True)
    v = jnp.var(x, axis=axis, keepdims=True)
    return (x - m) / jnp.sqrt(v + eps)

def _scatter_add(tgt, idx, src, axis=0):
    return tgt.at[idx].add(src)

def _segment_sum(src, seg, n):
    return jax.ops.segment_sum(src, seg, n)
kernel_name = 'mk_prb_d1_jaxref_r4_81859e'

def setup_inputs(seed: int=0):
    np.random.seed(seed)
    _w = jnp.asarray

    def _L0_attn_setup():
        import jax, jax.numpy as jnp
        import numpy as np
        H = 32
        HKV = 8
        D = 1024
        HD = D // H
        S = 256
        MASK_OUT = 0.9
        MIN_REMAIN = 128
        THETA = 10000.0

        def rope_tables(seq_len, hd):
            inv_freq = 1.0 / THETA ** (jnp.arange(0, hd, 2, dtype=jnp.float32) / hd)
            t = jnp.arange(seq_len, dtype=jnp.float32)
            freqs = jnp.outer(t, inv_freq)
            emb = jnp.concatenate([freqs, freqs], axis=-1)
            return (jnp.cos(emb), jnp.sin(emb))

        def rotate_half(x):
            x1, x2 = jnp.split(x, 2, axis=-1)
            return jnp.concatenate([-x2, x1], axis=-1)

        def apply_rope(x, cos, sin):
            return x * cos + rotate_half(x) * sin
        key = jax.random.key(seed)
        k0, k1, k2, k3, k4 = jax.random.split(key, 5)
        hidden_states = jax.random.normal(k0, (1, S, D), jnp.float32)
        Wq = jax.random.normal(k1, (D, D), jnp.float32) * 0.02
        Wk = jax.random.normal(k2, (HKV * HD, D), jnp.float32) * 0.02
        Wv = jax.random.normal(k3, (HKV * HD, D), jnp.float32) * 0.02
        Wo = jax.random.normal(k4, (D, D), jnp.float32) * 0.02
        return {'hidden_states': hidden_states, 'Wq': Wq, 'Wk': Wk, 'Wv': Wv, 'Wo': Wo}
    _L0_attn_in = _L0_attn_setup()

    def _L0_ffn_setup():
        import jax, jax.numpy as jnp
        import numpy as np
        NUM_EXPERTS = 8
        RANK = 32
        ALPHA = 16.0
        TOP_K = 2
        TEMPERATURE = 1.0
        GAMMA = 0.5
        SOFT_TOPK_TEMP = 0.5
        N_GRAM = 2
        EPS = 1e-06
        key = jax.random.key(seed)
        ks = jax.random.split(key, 6)
        d_in, d_out = (1024, 1024)
        Bsz, T = (4, 512)
        x = jax.random.normal(ks[0], (Bsz, T, d_in), dtype=jnp.float32)
        W = jax.random.normal(ks[1], (d_out, d_in), dtype=jnp.float32) / np.sqrt(d_in)
        b = jax.random.normal(ks[2], (d_out,), dtype=jnp.float32) * 0.01
        A = jax.random.normal(ks[3], (d_in, RANK), dtype=jnp.float32) / np.sqrt(d_in)
        Bmat = jax.random.normal(ks[4], (RANK, d_out), dtype=jnp.float32) * 0.01
        LiMEs = jax.random.normal(ks[5], (NUM_EXPERTS, RANK), dtype=jnp.float32) * 0.1
        return {'x': x, 'W': W, 'b': b, 'A': A, 'Bmat': Bmat, 'LiMEs': LiMEs}
    _L0_ffn_in = _L0_ffn_setup()
    _d = {'L0_attn_hidden_states': _L0_attn_in['hidden_states'], 'L0_attn_Wq': _L0_attn_in['Wq'], 'L0_attn_Wk': _L0_attn_in['Wk'], 'L0_attn_Wv': _L0_attn_in['Wv'], 'L0_attn_Wo': _L0_attn_in['Wo'], 'L0_ffn_W': _L0_ffn_in['W'], 'L0_ffn_b': _L0_ffn_in['b'], 'L0_ffn_A': _L0_ffn_in['A'], 'L0_ffn_Bmat': _L0_ffn_in['Bmat'], 'L0_ffn_LiMEs': _L0_ffn_in['LiMEs']}
    _x0 = _d['L0_attn_hidden_states']
    _d['L0_attn_hidden_states'] = jax.random.normal(jax.random.fold_in(jax.random.key(seed), 1), (1, 2048, 1024), dtype=_x0.dtype)
    del _x0
    return _d

def reference(L0_attn_hidden_states, L0_attn_Wq, L0_attn_Wk, L0_attn_Wv, L0_attn_Wo, L0_ffn_W, L0_ffn_b, L0_ffn_A, L0_ffn_Bmat, L0_ffn_LiMEs):

    def _L0_attn_ref(hidden_states, Wq, Wk, Wv, Wo):
        import jax, jax.numpy as jnp
        import numpy as np
        H = 32
        HKV = 8
        D = 1024
        HD = D // H
        S = 256
        MASK_OUT = 0.9
        MIN_REMAIN = 128
        THETA = 10000.0

        def rope_tables(seq_len, hd):
            inv_freq = 1.0 / THETA ** (jnp.arange(0, hd, 2, dtype=jnp.float32) / hd)
            t = jnp.arange(seq_len, dtype=jnp.float32)
            freqs = jnp.outer(t, inv_freq)
            emb = jnp.concatenate([freqs, freqs], axis=-1)
            return (jnp.cos(emb), jnp.sin(emb))

        def rotate_half(x):
            x1, x2 = jnp.split(x, 2, axis=-1)
            return jnp.concatenate([-x2, x1], axis=-1)

        def apply_rope(x, cos, sin):
            return x * cos + rotate_half(x) * sin
        B, Sq, Dm = hidden_states.shape
        dtype = hidden_states.dtype
        neg = jnp.finfo(dtype).min
        q = (hidden_states @ Wq.T).reshape(B, Sq, H, HD).transpose(0, 2, 1, 3)
        k = (hidden_states @ Wk.T).reshape(B, Sq, HKV, HD).transpose(0, 2, 1, 3)
        v = (hidden_states @ Wv.T).reshape(B, Sq, HKV, HD).transpose(0, 2, 1, 3)
        rep = H // HKV
        k = jnp.repeat(k, rep, axis=1)
        v = jnp.repeat(v, rep, axis=1)
        cos, sin = rope_tables(Sq, HD)
        qr = apply_rope(q, cos, sin)
        kr = apply_rope(k, cos, sin)
        draft = jnp.einsum('bhqd,bhkd->bhqk', qr, kr)
        qi = jnp.arange(Sq)
        ki = jnp.arange(Sq)
        causal_future = qi[:, None] < ki[None, :]
        draft = draft + jnp.where(causal_future, neg, jnp.asarray(0.0, dtype))
        num_remain = max(min(Sq, MIN_REMAIN), Sq - int(Sq * MASK_OUT))
        _, draft_indices = jax.lax.top_k(draft, num_remain)
        mask = jnp.full((B, H, Sq, Sq), neg, dtype)
        b_idx = jnp.arange(B)[:, None, None, None]
        h_idx = jnp.arange(H)[None, :, None, None]
        s_idx = jnp.arange(Sq)[None, None, :, None]
        mask = mask.at[b_idx, h_idx, s_idx, draft_indices].set(0.0)
        mask = jnp.where(causal_future[None, None, :, :], neg, mask)
        scores = jnp.einsum('bhqd,bhkd->bhqk', qr, kr) / np.sqrt(HD).astype(np.float32) + mask
        attn = jax.nn.softmax(scores, axis=-1)
        out = jnp.einsum('bhqk,bhkd->bhqd', attn, v)
        out = out.transpose(0, 2, 1, 3).reshape(B, Sq, Dm)
        return out @ Wo.T

    def _L0_ffn_ref(x, W, b, A, Bmat, LiMEs):
        import jax, jax.numpy as jnp
        import numpy as np
        NUM_EXPERTS = 8
        RANK = 32
        ALPHA = 16.0
        TOP_K = 2
        TEMPERATURE = 1.0
        GAMMA = 0.5
        SOFT_TOPK_TEMP = 0.5
        N_GRAM = 2
        EPS = 1e-06
        Bsz, T, d_in = x.shape
        E = LiMEs.shape[0]
        scaling = ALPHA / RANK
        H = jnp.einsum('btd,od->bto', x, W) + b
        z = jnp.einsum('btd,dr->btr', x, A)
        anchors = jnp.arange(N_GRAM - 1, T, N_GRAM)
        H_slice = H[:, anchors, :E]
        delta_slice = jnp.einsum('bar,er->bae', z[:, anchors], LiMEs)
        H_scale = jnp.maximum(jnp.max(jnp.abs(H_slice)), EPS)
        d_scale = jnp.maximum(jnp.max(jnp.abs(delta_slice)), EPS)
        logits = ((1.0 - GAMMA) * (H_slice / H_scale) + GAMMA * (delta_slice / d_scale)) / TEMPERATURE
        probs = jax.nn.softmax(logits, axis=-1)
        topk_vals, _ = jax.lax.top_k(probs, TOP_K)
        thresh = topk_vals[..., -1:]
        mask = jax.nn.sigmoid((probs - thresh) / SOFT_TOPK_TEMP)
        weights = probs * mask
        weights = weights / (jnp.sum(weights, axis=-1, keepdims=True) + 1e-09)
        weights_full = jnp.repeat(weights, N_GRAM, axis=1)
        p_mix = jnp.einsum('bte,er->btr', weights_full, LiMEs)
        delta = jnp.einsum('btr,ro->bto', z * p_mix, Bmat) * scaling
        return H + delta
    x = L0_attn_hidden_states
    xn = _layernorm(x, axis=-1)
    x = x + _L0_attn_ref(xn, L0_attn_Wq, L0_attn_Wk, L0_attn_Wv, L0_attn_Wo) + _L0_ffn_ref(xn, L0_ffn_W, L0_ffn_b, L0_ffn_A, L0_ffn_Bmat, L0_ffn_LiMEs)
    return x

_drawn_inputs = setup_inputs


def setup_inputs(seed=0):
    import zlib

    import numpy as np

    out = dict(_drawn_inputs(seed))
    spreads = {}
    factors = {'L0_attn_Wq': 3.041,
     'L0_attn_Wk': 2.834,
     'L0_ffn_b': 8.0,
     'L0_ffn_A': 8.0,
     'L0_ffn_Bmat': 8.0,
     'L0_ffn_LiMEs': 8.0}
    for name, (base, spread) in spreads.items():
        noise = np.random.default_rng([zlib.crc32(name.encode()), seed]).standard_normal(out[name].shape)
        drawn = base * np.exp(spread * noise) if base else spread * noise
        out[name] = jnp.asarray(drawn.astype(out[name].dtype))
    for name, factor in factors.items():
        out[name] = (out[name] * factor).astype(out[name].dtype)
    return out
```

```python
import math
from contextlib import ExitStack

import numpy as np

import concourse.bass as bass
from concourse import mybir

ALU = mybir.AluOpType
ACT = mybir.ActivationFunctionType
F32 = mybir.dt.float32
I32 = mybir.dt.int32
BF16 = mybir.dt.bfloat16
AX = mybir.AxisListType.X
RMAX = bass.bass_isa.ReduceOp.max

P = 128
S = 2048
D = 1024
C = D // P
T = S // P
HD = 32
G = 8
R = 4
RANK = 32
E = 8
A = P // 2
KEEP = max(min(S, 128), S - int(S * 0.9))
SCALE = float(np.float32(1) / np.float32(np.sqrt(HD)))
LN_EPS = 1e-5
BIG = 1e20
MASKED = -1e30

ROUNDS = 3
WINDOW = 8 * ROUNDS
AIM = KEEP + 8.5
NEAR = 4.0
PARTS = 8
CHUNK = 1024
MIDDLE = 512


PRIMED = 1


def semaphores(nc, ctx, primed):
    def sem(name):
        primed.append(ctx.enter_context(nc.semaphore(name)))
        return primed[-1]
    return sem


def prime(nc, sems):
    with nc.Block() as block:
        @block.sync
        def _(sp):
            for s in sems:
                sp.sem_inc(s, PRIMED)


def batches():
    return [0, 3, 5, 7, 9, 11, 13, 15, 14, 12, 10, 8, 6, 4, 2, 1]


def ordered(engine, sem):
    count = [0]

    def step(instruction):
        count[0] += 1
        instruction.then_inc(sem, 1)
        engine.wait_ge(sem, count[0])
    return step


def paced(engine, sem):
    count = [0]

    def put(instruction):
        count[0] += 1
        instruction.then_inc(sem, 1)

    def sync():
        engine.wait_ge(sem, count[0])
    return put, sync


def spread(ap, shape):
    return ap.broadcast_to(list(shape))


def tokens_program(nc, x, wv, a_in, w8, b8, lime_t, ident, xt_d, vt_d, z_keep, gate_in):
    with ExitStack() as ctx:
        sb = lambda n, s, d=F32: ctx.enter_context(nc.sbuf_tensor(n, s, d))
        primed = []
        sem = semaphores(nc, ctx, primed)
        pb = lambda n, s: ctx.enter_context(nc.psum_tensor(n, s, F32))
        wv_sb = sb("wv_sb", [P, C, G * HD])
        a_sb = sb("a_sb", [P, C, RANK])
        w8_sb = sb("w8_sb", [P, C, E])
        b8_sb = sb("b8_sb", [1, E])
        lt_sb = sb("lt_sb", [RANK, E])
        id_sb = sb("id_sb", [P, P])
        one_row = sb("one_row", [1, A])
        xin = sb("xin", [P, 2, D])
        xn = sb("xn", [P, 2, D])
        xt = sb("xt", [P, 2, C, P])
        vt = sb("vt", [P, 2, G, HD + 1])
        zt = sb("zt", [RANK, 2, P])
        stats = sb("stats", [P, 2, 6])
        mv = sb("mv", [P, 2])
        sd = sb("sd", [P, 1])
        rs = sb("rs", [P, 4])
        ps_t = pb("ps_t", [P, 2, C * P])
        ps_v = pb("ps_v", [P, 2, 512])
        ps_z = pb("ps_z", [P, 512])
        ps_g = pb("ps_g", [P, 512])

        weights_in = sem("weights_in")
        x_in = [sem("x_in0"), sem("x_in1")]
        var_ready = sem("var_ready")
        sd_ready = sem("sd_ready")
        xn_ready = sem("xn_ready")
        turned = sem("turned")
        xt_ready = sem("xt_ready")
        v_ready = sem("v_ready")
        z_ready = sem("z_ready")
        zt_ready = sem("zt_ready")
        gate_ready = sem("gate_ready")
        v_read = sem("v_read")
        gate_read = sem("gate_read")
        ones_ready = sem("ones_ready")
        stored = [sem("stored0"), sem("stored1")]
        chain = ctx.enter_context(nc.semaphore("chain"))
        prime(nc, primed)
        block = ctx.enter_context(nc.Block("tokens"))

        @block.sync
        def _(sp):
            for dst, src in ((id_sb, ident), (wv_sb, wv), (a_sb, a_in), (w8_sb, w8), (b8_sb, b8), (lt_sb, lime_t)):
                sp.dma_start(dst[:], src).then_inc(weights_in, 16)
            with sp.Fori(0, T // 2) as i:
                for h in range(2):
                    sp.wait_ge(xn_ready, PRIMED + 2 * i)
                    sp.dma_start(xin[:, h], x[2 * i + h]).then_inc(x_in[h], 16)
            for h in range(2):
                sp.wait_ge(stored[h], PRIMED + 32 * (T // 2))

        @block.gpsimd
        def _(pool):
            nc.gpsimd.memset(vt[:], 1.0).then_inc(ones_ready, 1)
            nc.gpsimd.memset(one_row[:], 1.0).then_inc(ones_ready, 1)

        @block.vector
        def _(dve):
            with dve.Fori(0, T // 2) as i:
                dve.sem_clear(chain)
                step = ordered(dve, chain)
                for h in range(2):
                    t = 2 * i + h
                    dve.wait_ge(x_in[h], PRIMED + 16 * i + 16)
                    nc.vector.bn_stats(stats[:, 0], xin[:, h, 0:D // 2])
                    step(nc.vector.bn_stats(stats[:, 1], xin[:, h, D // 2:D]))
                    step(nc.vector.bn_aggr(mv[:], stats[:]))
                    nc.vector.tensor_scalar(mv[:, 1:2], mv[:, 1:2], LN_EPS, None, ALU.add).then_inc(var_ready, 1)
                    dve.wait_ge(sd_ready, PRIMED + t + 1)
                    step(nc.vector.reciprocal(rs[:, 0:1], sd[:]))
                    step(nc.vector.scalar_tensor_tensor(rs[:, 1:2], rs[:, 0:1], rs[:, 0:1], mv[:, 1:2], ALU.mult, ALU.mult))
                    step(nc.vector.tensor_scalar(rs[:, 2:3], rs[:, 1:2], -0.5, 1.5, ALU.mult, ALU.add))
                    step(nc.vector.tensor_tensor(rs[:, 3:4], rs[:, 0:1], rs[:, 2:3], ALU.mult))
                    dve.wait_ge(turned, PRIMED + 2 * i)
                    nc.vector.tensor_scalar(xn[:, h], xin[:, h], mv[:, 0:1], rs[:, 3:4], ALU.subtract, ALU.mult).then_inc(xn_ready, 1)
                    dve.wait_ge(v_ready, PRIMED + t + 1)
                    dve.wait_ge(stored[h], PRIMED + 32 * i)
                    dve.wait_ge(ones_ready, PRIMED + 2)
                    nc.vector.tensor_copy(vt[:, h, :, 0:HD], ps_v[:, h, 0:G * HD].rearrange("p (g d) -> p g d", g=G)).then_inc(v_read, 1)
                    dve.wait_ge(gate_ready, PRIMED + t + 1)
                    nc.vector.tensor_copy(gate_in[:, bass.ds(t, 1)], ps_g[0:A, 0:2 * E]).then_inc(gate_read, 1)

        @block.scalar
        def _(act):
            with act.Fori(0, T // 2) as i:
                for h in range(2):
                    t = 2 * i + h
                    act.wait_ge(var_ready, PRIMED + t + 1)
                    nc.scalar.activation(sd[:], mv[:, 1:2], ACT.Sqrt).then_inc(sd_ready, 1)
                    act.wait_ge(turned, PRIMED + t + 1)
                    act.wait_ge(stored[h], PRIMED + 32 * i)
                    act.wait_ge(gate_ready, PRIMED + 2 * i)
                    nc.scalar.activation(xt[:, h], ps_t[:, h].rearrange("p (c k) -> p c k", c=C), ACT.Copy).then_inc(xt_ready, 1)
                    act.wait_ge(z_ready, PRIMED + t + 1)
                    nc.scalar.activation(zt[:, h], ps_z[0:RANK, 0:P], ACT.Copy).then_inc(zt_ready, 1)
                    nc.scalar.activation(z_keep[:, bass.ts(t, P)], ps_z[0:RANK, 0:P], ACT.Copy).then_inc(zt_ready, 1)
                    act.wait_ge(xt_ready, PRIMED + t + 1)
                    act.dma_start(xt_d[t], xt[:, h]).then_inc(stored[h], 16)
                    act.wait_ge(v_read, PRIMED + t + 1)
                    act.dma_start(vt_d[t], vt[:, h]).then_inc(stored[h], 16)

        @block.tensor
        def _(pe):
            pe.wait_ge(weights_in, PRIMED + 16 * 6)
            pe.wait_ge(ones_ready, PRIMED + 2)
            with pe.Fori(0, T // 2) as i:
                for h in range(2):
                    t = 2 * i + h
                    pe.wait_ge(xn_ready, PRIMED + t + 1)
                    pe.wait_ge(xt_ready, PRIMED + 2 * i)
                    for c in range(C):
                        mm = pe.transpose(ps_t[:, h, bass.ts(c, P)], xn[:, h, bass.ts(c, P)], id_sb[:])
                    mm.then_inc(turned, 1)
                    pe.wait_ge(xt_ready, PRIMED + t + 1)
                    pe.wait_ge(v_read, PRIMED + 2 * i)
                    for c in range(C):
                        mm = pe.matmul(ps_v[:, h, 0:G * HD], xt[:, h, c], wv_sb[:, c], start=(c == 0), stop=(c == C - 1))
                    mm.then_inc(v_ready, 1)
                    pe.wait_ge(zt_ready, PRIMED + 2 * t)
                    for c in range(C):
                        mm = pe.matmul(ps_z[0:RANK, 0:P], a_sb[:, c], xt[:, h, c], start=(c == 0), stop=(c == C - 1))
                    mm.then_inc(z_ready, 1)
                    pe.wait_ge(gate_read, PRIMED + t)
                    for c in range(C):
                        pe.matmul(ps_g[0:A, 0:E], xt[:, h, c, 1:P:2], w8_sb[:, c], start=(c == 0), stop=False, skip_group_check=True)
                    pe.matmul(ps_g[0:A, 0:E], one_row[:], b8_sb[:], start=False, stop=True, skip_group_check=True)
                    pe.wait_ge(zt_ready, PRIMED + 2 * t + 2)
                    pe.matmul(ps_g[0:A, E:2 * E], zt[:, h, 1:P:2], lt_sb[:], start=False, stop=True, skip_group_check=True).then_inc(gate_ready, 1)


def router_program(nc, lime, ident, zp_d, z_keep, gate_in):
    with ExitStack() as ctx:
        sb = lambda n, s, d=F32: ctx.enter_context(nc.sbuf_tensor(n, s, d))
        primed = []
        sem = semaphores(nc, ctx, primed)
        lm_sb = sb("lm_sb", [E, RANK])
        id_sb = sb("rt_id_sb", [P, P])
        peak = sb("peak", [A, 2])
        peak_all = sb("peak_all", [A, 2])
        half = sb("half", [A, 2])
        lg = sb("lg", [A, T, E])
        lg2 = sb("lg2", [A, T, E])
        sig = sb("sig", [A, T, E])
        row = sb("row", [A, T])
        row2 = sb("row2", [A, T])
        top = sb("top", [A, T, 8])
        wt = sb("wt", [E, T * A])
        zp = sb("zp", [RANK + 1, S])
        ps_w = ctx.enter_context(nc.psum_tensor("ps_w", [P, 2, 512], F32))
        ps_m = ctx.enter_context(nc.psum_tensor("ps_m", [P, 2, 512], F32))
        loaded = sem("rt_loaded")
        peak_ready = sem("peak_ready")
        peak_shared = sem("peak_shared")
        logits_ready = sem("logits_ready")
        exp_ready = sem("rt_exp_ready")
        probs_ready = sem("rt_probs_ready")
        sig_ready = sem("sig_ready")
        weights_ready = sem("weights_ready")
        turned = sem("rt_turned")
        wt_ready = sem("wt_ready")
        mix_ready = sem("mix_ready")
        zp_ready = sem("zp_ready")
        stored = sem("rt_stored")
        chain = ctx.enter_context(nc.semaphore("rt_chain"))
        prime(nc, primed)
        block = ctx.enter_context(nc.Block("router"))
        per_row = lambda ap: spread(ap[:].unsqueeze(2), [A, T, E])

        @block.sync
        def _(sp):
            sp.dma_start(lm_sb[:], lime).then_inc(loaded, 16)
            sp.dma_start(id_sb[:], ident).then_inc(loaded, 16)
            sp.wait_ge(zp_ready, PRIMED + 1)
            sp.dma_start(zp_d, zp[:]).then_inc(stored, 16)
            sp.wait_ge(stored, PRIMED + 16)

        @block.gpsimd
        def _(pool):
            pool.wait_ge(peak_ready, PRIMED + 1)
            nc.gpsimd.partition_all_reduce(peak_all[:], peak[:], A, RMAX).then_inc(peak_shared, 1)

        @block.scalar
        def _(act):
            act.wait_ge(logits_ready, PRIMED + 1)
            nc.scalar.activation(lg[:], lg2[:], ACT.Exp).then_inc(exp_ready, 1)
            act.wait_ge(probs_ready, PRIMED + 1)
            nc.scalar.activation(sig[:], lg2[:], ACT.Exp, scale=-2.0).then_inc(sig_ready, 1)

        @block.tensor
        def _(pe):
            pe.wait_ge(loaded, PRIMED + 32)
            pe.wait_ge(weights_ready, PRIMED + 1)
            for t in range(T):
                mm = pe.transpose(ps_w[0:E, t // 8, bass.ts(t % 8, A)], lg[:, t], id_sb[0:A, 0:A])
            mm.then_inc(turned, 1)
            pe.wait_ge(wt_ready, PRIMED + 1)
            for j in range(2):
                mm = pe.matmul(ps_m[0:RANK, j], lm_sb[:], wt[:, bass.ts(j, 512)], start=True, stop=True)
            mm.then_inc(mix_ready, 1)

        @block.vector
        def _(dve):
            step = ordered(dve, chain)
            V = nc.vector
            step(V.memset(zp[:], 1.0))
            for n in range(2):
                part = gate_in[:, :, bass.ts(n, E)]
                step(V.scalar_tensor_tensor(lg[:], part, -1.0, part, ALU.mult, ALU.max))
                last = V.tensor_reduce(peak[:, n:n + 1], lg[:].rearrange("p t e -> p (t e)"), AX, ALU.max)
                if n == 0:
                    step(last)
                else:
                    last.then_inc(peak_ready, 1)
            dve.wait_ge(peak_shared, PRIMED + 1)
            step(V.tensor_scalar(half[:], peak_all[:], 1e-6, None, ALU.max))
            step(V.reciprocal(peak[:], half[:]))
            step(V.tensor_scalar(half[:], peak[:], 0.5, None, ALU.mult))
            step(V.tensor_scalar(lg[:], gate_in[:, :, E:2 * E], half[:, 1:2], None, ALU.mult))
            step(V.scalar_tensor_tensor(lg[:], gate_in[:, :, 0:E], half[:, 0:1], lg[:], ALU.mult, ALU.add))
            step(V.tensor_reduce(row[:], lg[:], AX, ALU.max))
            V.tensor_tensor(lg2[:], lg[:], per_row(row), ALU.subtract).then_inc(logits_ready, 1)
            dve.wait_ge(exp_ready, PRIMED + 1)
            step(V.tensor_reduce(row[:], lg[:], AX, ALU.add))
            step(V.reciprocal(row2[:], row[:]))
            step(V.tensor_tensor(lg[:], lg[:], per_row(row2), ALU.mult))
            for t in range(T):
                last = V.max(top[:, t], lg[:, t])
            step(last)
            V.tensor_tensor(lg2[:], lg[:], spread(top[:, :, 1:2], [A, T, E]), ALU.subtract).then_inc(probs_ready, 1)
            dve.wait_ge(sig_ready, PRIMED + 1)
            step(V.tensor_scalar(sig[:], sig[:], 1.0, None, ALU.add))
            step(V.reciprocal(lg2[:], sig[:]))
            step(V.tensor_tensor(lg2[:], lg2[:], lg[:], ALU.mult))
            step(V.tensor_reduce(row[:], lg2[:], AX, ALU.add))
            step(V.tensor_scalar(row[:], row[:], 1e-9, None, ALU.add))
            step(V.reciprocal(row2[:], row[:]))
            V.tensor_tensor(lg[:], lg2[:], per_row(row2), ALU.mult).then_inc(weights_ready, 1)
            dve.wait_ge(turned, PRIMED + 1)
            nc.vector.tensor_copy(wt[:].rearrange("e (j n) -> e j n", j=2), ps_w[0:E]).then_inc(wt_ready, 1)
            dve.wait_ge(mix_ready, PRIMED + 1)
            V.scalar_tensor_tensor(
                zp[0:RANK].rearrange("r (a n) -> r a n", n=2), z_keep[:].rearrange("r (a n) -> r a n", n=2), 0.5,
                spread(ps_m[0:RANK].rearrange("r j n -> r (j n)").unsqueeze(2), [RANK, S // 2, 2]),
                ALU.mult, ALU.mult).then_inc(zp_ready, 1)


def heads_program(nc, wqk, xt_d, cos, sin, rot_t, ident, block_mean, head_sel, zrow, qk_d, stat_d):
    with ExitStack() as ctx:
        sb = lambda n, s, d=F32: ctx.enter_context(nc.sbuf_tensor(n, s, d))
        primed = []
        sem = semaphores(nc, ctx, primed)
        pb = lambda n, s: ctx.enter_context(nc.psum_tensor(n, s, F32))
        xt = sb("h_xt", [P, T, C, P])
        w_sb = sb("w_sb", [P, 2, C, 2 * P])
        cos_sb = sb("cos_sb", [P, S])
        sin_sb = sb("sin_sb", [P, S])
        rot_sb = sb("rot_sb", [P, P])
        id_sb = sb("h_id_sb", [P, P])
        bm_sb = sb("bm_sb", [P, P])
        hs_sb = sb("hs_sb", [P, R])
        zr_sb = sb("zr_sb", [P, 3, T * R])
        raw = sb("raw", [P, 2, 512])
        tmp = sb("tmp", [P, 2, 512])
        qk = sb("qk", [P, 2, S])
        krow = sb("krow", [P, 2, P])
        cb = sb("cb", [P, P])
        km = sb("km", [P, 1])
        kmb = sb("kmb", [P, R])
        prod = sb("prod", [P, S])
        stat = sb("stat", [P, 2, T * R])
        sg = sb("sg", [P, 4, T * R])
        ps_p = pb("ps_p", [P, 2, 512])
        ps_r = pb("ps_r", [P, 2, 512])
        ps_k = pb("ps_k", [P, 2, 512])
        ps_c = pb("ps_c", [P, 512])
        ps_s = pb("ps_s", [P, 512])

        consts_in = sem("h_consts_in")
        x_in = sem("h_x_in")
        w_in = [sem("w_in0"), sem("w_in1")]
        proj_ready = sem("proj_ready")
        raw_ready = sem("raw_ready")
        rot_ready = sem("rot_ready")
        part_ready = sem("part_ready")
        krow_turned = sem("krow_turned")
        krow_ready = sem("krow_ready")
        krow_used = sem("krow_used")
        moments_used = sem("moments_used")
        moment_prod = sem("moment_prod")
        prod_ready = sem("prod_ready")
        square_ready = sem("square_ready")
        var_ready = sem("h_var_ready")
        dev_ready = sem("dev_ready")
        stat_ready = sem("stat_ready")
        stored = sem("h_stored")
        chain = ctx.enter_context(nc.semaphore("h_chain"))
        prime(nc, primed)
        block = ctx.enter_context(nc.Block("heads"))
        UNITS = 8

        @block.sync
        def _(sp):
            for dst, src in ((rot_sb, rot_t), (id_sb, ident), (bm_sb, block_mean), (hs_sb, head_sel), (zr_sb, zrow),
                             (cos_sb, cos), (sin_sb, sin)):
                sp.dma_start(dst[:], src).then_inc(consts_in, 16)
            for n in range(4):
                sp.dma_start(xt[:, 4 * n:4 * n + 4], xt_d[4 * n:4 * n + 4].rearrange("t p c k -> p t c k")).then_inc(x_in, 16)
            with sp.Fori(0, G // 2) as i:
                for h in range(2):
                    g = 2 * i + h
                    sp.wait_ge(proj_ready, PRIMED + 2 * UNITS * i)
                    sp.dma_start(w_sb[:, h], wqk[g]).then_inc(w_in[h], 16)
                for h in range(2):
                    g = 2 * i + h
                    sp.wait_ge(part_ready, PRIMED + UNITS * g + 4)
                    sp.dma_start(qk_d[g, 0], qk[:, 0]).then_inc(stored, 16)
                    sp.wait_ge(part_ready, PRIMED + UNITS * g + 8)
                    sp.dma_start(qk_d[g, 1], qk[:, 1]).then_inc(stored, 16)
                    sp.wait_ge(stat_ready, PRIMED + g + 1)
                    sp.dma_start(stat_d[g], stat[:]).then_inc(stored, 16)
            sp.wait_ge(stored, PRIMED + 48 * G)

        @block.tensor
        def _(pe):
            pe.wait_ge(consts_in, PRIMED + 16 * 7)
            pe.wait_ge(x_in, PRIMED + 64)
            with pe.Fori(0, G // 2) as i:
                for h in range(2):
                    g = 2 * i + h
                    pe.wait_ge(w_in[h], PRIMED + 16 * i + 16)

                    def project(u):
                        which, j = u // 4, u % 4
                        if u < 2:
                            pe.wait_ge(raw_ready, PRIMED + UNITS * g)
                        else:
                            pe.wait_ge(raw_ready, PRIMED + UNITS * g + u - 1)
                        for c in range(C):
                            mm = pe.matmul(ps_p[:, u % 2], w_sb[:, h, c, bass.ts(which, P)],
                                           xt[:, 4 * j:4 * j + 4, c], start=(c == 0), stop=(c == C - 1))
                        mm.then_inc(proj_ready, 1)

                    def turn(u):
                        pe.wait_ge(raw_ready, PRIMED + UNITS * g + u + 1)
                        if u < 2:
                            pe.wait_ge(part_ready, PRIMED + UNITS * g)
                        else:
                            pe.wait_ge(part_ready, PRIMED + UNITS * g + u - 1)
                        pe.matmul(ps_r[:, u % 2], rot_sb[:], raw[:, u % 2], start=True, stop=True).then_inc(rot_ready, 1)

                    def k_rows(u):
                        pe.wait_ge(part_ready, PRIMED + UNITS * g + u + 1)
                        for n in range(4 * u, 4 * u + 4):
                            if n >= 2:
                                pe.wait_ge(krow_ready, PRIMED + T * g + n - 1)
                            else:
                                pe.wait_ge(krow_ready, PRIMED + T * g)
                            pe.transpose(ps_k[:, n % 2, 0:P], qk[:, 0, bass.ts(n, P)], id_sb[:]).then_inc(krow_turned, 1)
                            if n > 0:
                                moments(n - 1)

                    def moments(n):
                        pe.wait_ge(krow_ready, PRIMED + T * g + n + 1)
                        if n == 0:
                            pe.wait_ge(moments_used, PRIMED + g)
                        pe.matmul(ps_c[:, 0:P], krow[:, n % 2], krow[:, n % 2], start=(n == 0), stop=(n == T - 1)).then_inc(krow_used, 1)

                    for u in range(UNITS):
                        project(u)
                        if u:
                            turn(u - 1)
                        if 2 <= u < 6:
                            k_rows(u - 2)
                    turn(UNITS - 1)
                    moments(T - 1)
                    pe.wait_ge(moments_used, PRIMED + g + 1)
                    for j in range(4):
                        pe.wait_ge(part_ready, PRIMED + UNITS * g + 4 + j + 1)
                        pe.wait_ge(raw_ready, PRIMED + UNITS * g + UNITS)
                        if j >= 2:
                            pe.wait_ge(prod_ready, PRIMED + 4 * g + j - 1)
                        pe.matmul(ps_p[:, j % 2], cb[:], qk[:, 1, bass.ts(j, 512)], start=True, stop=True).then_inc(moment_prod, 1)
                    pe.wait_ge(prod_ready, PRIMED + 4 * g + 4)
                    pe.wait_ge(stat_ready, PRIMED + g)
                    for t in range(T):
                        pe.matmul(ps_s[:, bass.ts(t, R)], prod[:, bass.ts(t, P)], hs_sb[:], start=(t == 0), stop=True, skip_group_check=True)
                        mm = pe.matmul(ps_s[:, bass.ds(T * R + t * R, R)], qk[:, 1, bass.ts(t, P)], kmb[:], start=False, stop=True, skip_group_check=True)
                    mm.then_inc(square_ready, 1)

        @block.scalar
        def _(act):
            with act.Fori(0, G) as g:
                def copy_raw(u):
                    act.wait_ge(proj_ready, PRIMED + UNITS * g + u + 1)
                    act.wait_ge(part_ready, PRIMED + UNITS * g + u - 1) if u >= 2 else act.wait_ge(part_ready, PRIMED + UNITS * g)
                    nc.scalar.activation(raw[:, u % 2], ps_p[:, u % 2], ACT.Copy).then_inc(raw_ready, 1)

                def copy_rows(u):
                    for n in range(4 * u, 4 * u + 4):
                        act.wait_ge(krow_turned, PRIMED + T * g + n + 1)
                        act.wait_ge(krow_used, PRIMED + T * g + n - 1) if n >= 2 else act.wait_ge(krow_used, PRIMED + T * g)
                        nc.scalar.activation(krow[:, n % 2], ps_k[:, n % 2, 0:P], ACT.Copy).then_inc(krow_ready, 1)

                for u in range(UNITS):
                    if u == 0:
                        act.wait_ge(prod_ready, PRIMED + 4 * g)
                    copy_raw(u)
                    if 2 <= u < 6:
                        copy_rows(u - 2)
                act.wait_ge(var_ready, PRIMED + g + 1)
                nc.scalar.activation(sg[:, 2], sg[:, 1], ACT.Sqrt).then_inc(dev_ready, 1)

        @block.vector
        def _(dve):
            V = nc.vector
            dve.wait_ge(consts_in, PRIMED + 16 * 7)
            with dve.Fori(0, G) as g:
                dve.sem_clear(chain)
                step = ordered(dve, chain)
                dve.wait_ge(stored, PRIMED + 48 * g)
                for u in range(UNITS):
                    which, j = u // 4, u % 4
                    cols = bass.ts(j, 512)
                    dve.wait_ge(raw_ready, PRIMED + UNITS * g + u + 1)
                    V.tensor_tensor(tmp[:, 0], raw[:, u % 2], cos_sb[:, cols], ALU.mult)
                    dve.wait_ge(rot_ready, PRIMED + UNITS * g + u + 1)
                    step(V.tensor_tensor(tmp[:, 1], ps_r[:, u % 2], sin_sb[:, cols], ALU.mult))
                    V.tensor_tensor(qk[:, which, cols], tmp[:, 0], tmp[:, 1], ALU.add).then_inc(part_ready, 1)
                    dve.wait_ge(part_ready, PRIMED + UNITS * g + u + 1)
                step(V.tensor_reduce(km[:], qk[:, 0], AX, ALU.add))
                step(V.tensor_scalar(kmb[:], hs_sb[:], km[:, 0:1], SCALE / S, ALU.mult, ALU.mult))
                dve.wait_ge(krow_used, PRIMED + T * g + T)
                V.tensor_tensor(cb[:], ps_c[:, 0:P], bm_sb[:], ALU.mult).then_inc(moments_used, 1)
                for j in range(4):
                    dve.wait_ge(moment_prod, PRIMED + 4 * g + j + 1)
                    V.tensor_tensor(prod[:, bass.ts(j, 512)], ps_p[:, j % 2], qk[:, 1, bass.ts(j, 512)], ALU.mult).then_inc(prod_ready, 1)
                dve.wait_ge(square_ready, PRIMED + g + 1)
                n = T * R
                step(V.tensor_copy(sg[:, 0], ps_s[:, n:2 * n]))
                step(V.tensor_tensor(sg[:, 3], sg[:, 0], sg[:, 0], ALU.mult))
                step(V.tensor_tensor(sg[:, 1], ps_s[:, 0:n], sg[:, 3], ALU.subtract))
                V.tensor_scalar(sg[:, 1], sg[:, 1], 0.0, None, ALU.max).then_inc(var_ready, 1)
                dve.wait_ge(dev_ready, PRIMED + g + 1)
                step(V.tensor_tensor(stat[:, 0], sg[:, 2], zr_sb[:, 0], ALU.mult))
                step(V.tensor_tensor(stat[:, 0], stat[:, 0], sg[:, 0], ALU.add))
                step(V.tensor_tensor(stat[:, 0], stat[:, 0], zr_sb[:, 1], ALU.add))
                V.tensor_tensor(stat[:, 1], sg[:, 2], zr_sb[:, 2], ALU.mult).then_inc(stat_ready, 1)
                dve.wait_ge(stat_ready, PRIMED + g + 1)


class Plan:

    def __init__(self):
        self.tile = batches()
        self.keys = [P * (b + 1) for b in self.tile]
        self.chunks = [R * -(-n // CHUNK) for n in self.keys]
        before = lambda xs: [sum(xs[:i]) for i in range(len(xs) + 1)]
        self.chunk0 = before(self.chunks)
        self.block0 = before([b + 1 for b in self.tile])
        self.search = [int(n > KEEP) for n in self.keys]
        self.search0 = before(self.search)
        self.n = len(self.tile)


def attention_program(nc, qk_d, vt_d, stat_d, at_d, ident, ident_bf, causal_bf, bits, ranks, floors):
    plan = Plan()
    NB = plan.n
    CH, BL, SE = plan.chunk0[NB], plan.block0[NB], plan.search0[NB]
    assert CH % 2 == 0 and BL % 2 == 0
    with ExitStack() as ctx:
        sb = lambda n, s, d=F32: ctx.enter_context(nc.sbuf_tensor(n, s, d))
        primed = []
        sem = semaphores(nc, ctx, primed)
        pb = lambda n, s: ctx.enter_context(nc.psum_tensor(n, s, F32))
        qt = sb("at_qt", [P, S])
        kt = sb("at_kt", [P, S])
        v_sb = sb("v_sb", [P, T, HD + 1])
        guess = sb("guess", [P, 2, T, R])
        gap = sb("gap", [P, 3, R, S])
        prob = sb("prob", [P, 2, R, S])
        near = sb("near", [P, S])
        junk = sb("junk", [P, S], BF16)
        pt = sb("pt", [P, 2, R * P])
        id_sb = sb("at_id_sb", [P, P])
        idb_words = sb("idb_sb", [P, P // 2], I32)
        idb_sb = idb_words[:].bitcast(BF16)
        cz_words = sb("cz_sb", [P, P // 2], I32)
        cz_sb = cz_words[:].bitcast(BF16)
        bits_sb = sb("bits_sb", [P, 31], I32)
        rank_sb = sb("rank_sb", [P, R, WINDOW])
        floor_sb = sb("floor_sb", [P, 2])
        ones = sb("at_ones", [P, 1])
        part_max = sb("part_max", [P, R, 2])
        row_max = sb("row_max", [P, 2, R])
        thr = sb("thr", [P, 3, R])
        sums = sb("sums", [P, 2, 3, R])
        upd = sb("upd", [P, 5, R])
        miss = sb("miss", [P, 2, R])
        cand = sb("cand", [P, R, PARTS, 8])
        cand2 = sb("cand2", [P, 2, R, PARTS * 8])
        best = sb("best", [P, R, WINDOW])
        hit = sb("hit", [P, R, WINDOW])
        small = sb("small", [P, 6, R])
        cut = sb("cut", [P, 2, R])
        bad = sb("bad", [P, R])
        flag = sb("flag", [1, 1], I32)
        flag_at = sb("flag_at", [1, 1], I32)
        f_bits = sb("f_bits", [P, R], I32)
        f_try = sb("f_try", [P, R], I32)
        f_mask = sb("f_mask", [P, R], I32)
        f_count = sb("f_count", [P, R])
        rden = sb("rden", [P, R])
        o_sb = sb("o_sb", [P, P])
        ot = sb("ot", [P, 2, P])
        ps_s = pb("at_ps_s", [P, 2, CHUNK])
        ps_t = pb("at_ps_t", [P, 2, 512])
        ps_o = pb("at_ps_o", [P, 512])
        ps_x = pb("at_ps_x", [P, 512])

        consts_in = sem("at_consts_in")
        ones_ready = sem("at_ones_ready")
        qk_in = sem("qk_in")
        v_in = sem("v_in")
        guess_in = sem("guess_in")
        scores_ready = sem("scores_ready")
        scores_read = sem("scores_read")
        max_ready = sem("max_ready")
        gap_ready = sem("gap_ready")
        pool_turns = sem("pool_turns")
        thr_ready = [sem(f"thr_ready{n}") for n in range(3)]
        probed = sem("probed")
        exp_ready = sem("exp_ready")
        kept_ready = sem("kept_ready")
        bad_ready = sem("bad_ready")
        flag_ready = sem("flag_ready")
        flag_read = sem("flag_read")
        pt_turned = sem("pt_turned")
        pt_ready = sem("pt_ready")
        pv_done = sem("pv_done")
        out_ready = sem("out_ready")
        ot_turned = sem("ot_turned")
        ot_ready = sem("ot_ready")
        ot_stored = [sem("ot_stored0"), sem("ot_stored1")]
        chain = ctx.enter_context(nc.semaphore("at_chain"))
        fchain = ctx.enter_context(nc.semaphore("fchain"))
        prime(nc, primed)
        block = ctx.enter_context(nc.Block("attention"))

        def pieces(s):
            out, n = [], plan.chunk0[s]
            for r in range(R):
                for k0 in range(0, plan.keys[s], CHUNK):
                    out.append((r, k0, min(CHUNK, plan.keys[s] - k0), n))
                    n += 1
            return out

        def thirds(s):
            n = plan.tile[s] + 1
            return [range(0, n // 2), range(n // 2, 3 * n // 4), range(3 * n // 4, n)]

        @block.sync
        def _(sp):
            for dst, src in ((id_sb, ident), (idb_words, ident_bf), (cz_words, causal_bf), (bits_sb, bits), (rank_sb, ranks),
                             (floor_sb, floors)):
                sp.dma_start(dst[:], src).then_inc(consts_in, 16)
            with sp.Fori(0, G) as g:
                sp.wait_ge(scores_ready, PRIMED + CH * g)
                sp.dma_start(kt[:], qk_d[g, 0]).then_inc(qk_in, 16)
                sp.dma_start(qt[:], qk_d[g, 1]).then_inc(qk_in, 16)
                sp.wait_ge(thr_ready[2], PRIMED + SE * g)
                sp.dma_start(guess[:], stat_d[g].rearrange("p a (t r) -> p a t r", r=R)).then_inc(guess_in, 16)
                sp.wait_ge(pv_done, PRIMED + BL * g)
                sp.dma_start(v_sb[:], vt_d[:, :, g].rearrange("t p d -> p t d")).then_inc(v_in, 16)
                for s in range(NB):
                    sp.wait_ge(ot_ready, PRIMED + NB * g + s + 1)
                    sp.dma_start(at_d[plan.tile[s], :, g], ot[:, s % 2]).then_inc(ot_stored[s % 2], 16)
            for h in range(2):
                sp.wait_ge(ot_stored[h], PRIMED + 16 * G * NB // 2)

        @block.gpsimd
        def _(pool):
            nc.gpsimd.memset(ones[:], 1.0).then_inc(ones_ready, 1)
            with pool.Fori(0, G) as g:
                for s in range(NB):
                    n = plan.keys[s]
                    pool.wait_ge(max_ready, PRIMED + NB * g + s + 1)
                    pool.sem_inc(pool_turns)
                    for r in range(R):
                        nc.gpsimd.tensor_scalar(gap[:, s % 3, r, 0:n], gap[:, s % 3, r, 0:n], -1.0,
                                                row_max[:, s % 2, r:r + 1], ALU.mult, ALU.add).then_inc(gap_ready, 1)

        @block.tensor
        def _(pe):
            pe.wait_ge(consts_in, PRIMED + 16 * 6)
            pe.wait_ge(ones_ready, PRIMED + 1)
            with pe.Fori(0, G) as g:
                def scores(s, piece):
                    r, k0, n, ch = piece
                    q0 = P * plan.tile[s]
                    rows = slice(HD * r, HD * r + HD)
                    pe.wait_ge(scores_read, PRIMED + CH * g + (ch - 1 if ch >= 2 else 0))
                    for k in range(0, n, 512):
                        w = min(512, n - k)
                        diagonal = k0 + k + w == plan.keys[s]
                        mm = pe.matmul(ps_s[:, ch % 2, k:k + w], qt[rows, q0:q0 + P], kt[rows, k0 + k:k0 + k + w],
                                       start=True, stop=not diagonal, skip_group_check=True)
                        if diagonal:
                            mm = pe.matmul(ps_s[:, ch % 2, k + w - P:k + w], idb_sb, cz_sb,
                                           start=False, stop=True, skip_group_check=True)
                    mm.then_inc(scores_ready, 1)

                def turn_block(s, j):
                    b = plan.block0[s] + j
                    if plan.search[s]:
                        if j == 0:
                            pe.wait_ge(kept_ready, PRIMED + R * SE * g + R * plan.search0[s] + R)
                    elif j == 0:
                        pe.wait_ge(exp_ready, PRIMED + R * NB * g + R * s + R)
                    pe.wait_ge(pt_ready, PRIMED + BL * g + (b - 1 if b >= 2 else 0))
                    for r in range(R):
                        mm = pe.transpose(ps_t[:, b % 2, bass.ts(r, P)], prob[:, s % 2, r, bass.ts(j, P)], id_sb[:])
                    mm.then_inc(pt_turned, 1)

                def times_v(s, j):
                    b = plan.block0[s] + j
                    pe.wait_ge(pt_ready, PRIMED + BL * g + b + 1)
                    if j == 0:
                        pe.wait_ge(out_ready, PRIMED + NB * g + s)
                    for r in range(R):
                        mm = pe.matmul(ps_o[:, (HD + 1) * r:(HD + 1) * (r + 1)], pt[:, b % 2, bass.ts(r, P)], v_sb[:, j],
                                       start=(j == 0 and r == 0), stop=(j == plan.tile[s]), skip_group_check=True)
                    mm.then_inc(pv_done, 1)

                def blocks(s, run, between=()):
                    between = list(between)
                    for j in run:
                        turn_block(s, j)
                        if j > run.start:
                            times_v(s, j - 1)
                        take = -(-len(between) // (run.stop - j))
                        for piece in between[:take]:
                            scores(*piece)
                        between = between[take:]
                    if run:
                        times_v(s, run.stop - 1)
                    for piece in between:
                        scores(*piece)

                def turn_out(s):
                    pe.wait_ge(out_ready, PRIMED + NB * g + s + 1)
                    if s:
                        pe.wait_ge(ot_ready, PRIMED + NB * g + s)
                    pe.transpose(ps_x[:, P:2 * P], o_sb[:], id_sb[:]).then_inc(ot_turned, 1)

                def raise_flag(s):
                    n = SE * g + plan.search0[s]
                    pe.wait_ge(bad_ready, PRIMED + n + 1)
                    pe.matmul(ps_x[0:1, 0:R], ones[:], bad[:], start=True, stop=True).then_inc(flag_ready, 1)

                pe.wait_ge(qk_in, PRIMED + 32 * g + 32)
                pe.wait_ge(v_in, PRIMED + 16 * g + 16)
                for piece in pieces(0):
                    scores(0, piece)
                for k in range(NB + 3):
                    ahead = [(k + 1, p) for p in pieces(k + 1)] if k + 1 < NB else []
                    if 0 <= k - 2 < NB:
                        blocks(k - 2, thirds(k - 2)[0], ahead)
                    else:
                        for piece in ahead:
                            scores(*piece)
                    if 0 <= k - 3 < NB:
                        if 0 <= k - 2 < NB and plan.search[k - 2]:
                            pe.wait_ge(flag_read, PRIMED + SE * g + plan.search0[k - 2] + 1)
                        turn_out(k - 3)
                    if 0 <= k - 1 < NB and plan.search[k - 1]:
                        if 0 <= k - 3:
                            pe.wait_ge(ot_ready, PRIMED + NB * g + k - 2)
                        raise_flag(k - 1)
                    if 0 <= k - 2 < NB:
                        blocks(k - 2, thirds(k - 2)[1])
                        blocks(k - 2, thirds(k - 2)[2])

        @block.scalar
        def _(act):
            with act.Fori(0, G) as g:
                def copy_block(s, j):
                    b = plan.block0[s] + j
                    act.wait_ge(pt_turned, PRIMED + BL * g + b + 1)
                    act.wait_ge(pv_done, PRIMED + BL * g + (b - 1 if b >= 2 else 0))
                    nc.scalar.activation(pt[:, b % 2], ps_t[:, b % 2], ACT.Copy).then_inc(pt_ready, 1)

                def probe(s, n, r):
                    m = SE * g + plan.search0[s]
                    if r == 0:
                        act.wait_ge(thr_ready[n], PRIMED + m + 1)
                    if n == 0:
                        act.wait_ge(gap_ready, PRIMED + R * NB * g + R * s + r + 1)
                    N = plan.keys[s]
                    act.wait_ge(probed, PRIMED + 3 * R * m + R * n + r)
                    nc.scalar.activation(junk[:, 0:N], gap[:, s % 3, r, 0:N], ACT.Sign, bias=thr[:, s % 3, r:r + 1], scale=-1.0,
                                         accum_out=sums[:, s % 2, n, r:r + 1]).then_inc(probed, 1)

                def weights(s, r):
                    N = plan.keys[s]
                    if not plan.search[s]:
                        act.wait_ge(gap_ready, PRIMED + R * NB * g + R * s + r + 1)
                    nc.scalar.activation(prob[:, s % 2, r, 0:N], gap[:, s % 3, r, 0:N], ACT.Exp, scale=-1.0).then_inc(exp_ready, 1)

                def copy_out(s):
                    act.wait_ge(ot_turned, PRIMED + NB * g + s + 1)
                    act.wait_ge(ot_stored[s % 2], PRIMED + (NB // 2) * 16 * g + 16 * (s // 2))
                    nc.scalar.activation(ot[:, s % 2], ps_x[:, P:2 * P], ACT.Copy).then_inc(ot_ready, 1)

                for k in range(NB + 3):
                    runs = thirds(k - 2) if 0 <= k - 2 < NB else [(), (), ()]
                    here = 0 <= k < NB and plan.search[k]
                    probes = [[lambda r=r, n=n: probe(k, n, r) for r in range(R)] if here else [] for n in range(3)]
                    if 0 <= k - 1 < NB:
                        probes[0] += [lambda r=r: weights(k - 1, r) for r in range(R)]
                    for n in range(3):
                        left = list(runs[n])
                        for m, item in enumerate(probes[n]):
                            item()
                            take = -(-len(left) // (len(probes[n]) - m))
                            for j in left[:take]:
                                copy_block(k - 2, j)
                            left = left[take:]
                        for j in left:
                            copy_block(k - 2, j)
                        if n == 0 and 0 <= k - 3 < NB:
                            copy_out(k - 3)

        @block.vector
        def _(dve):
            V = nc.vector
            dve.wait_ge(consts_in, PRIMED + 16 * 6)
            with dve.Fori(0, G) as g:
                dve.sem_clear(chain)
                put, sync = paced(dve, chain)

                def step(instruction):
                    put(instruction)
                    sync()

                def read_scores(s, piece):
                    r, k0, n, ch = piece
                    dve.wait_ge(scores_ready, PRIMED + CH * g + ch + 1)
                    V.tensor_scalar(gap[:, s % 3, r, k0:k0 + n], ps_s[:, ch % 2, 0:n], SCALE, None, ALU.mult, ALU.max,
                                    accum_out=part_max[:, r, k0 // CHUNK:k0 // CHUNK + 1]).then_inc(scores_read, 1)

                def first_guess(s):
                    dve.wait_ge(scores_read, PRIMED + CH * g + plan.chunk0[s + 1])
                    if plan.chunks[s] > R:
                        last = V.tensor_reduce(row_max[:, s % 2], part_max[:], AX, ALU.max)
                    else:
                        last = V.tensor_copy(row_max[:, s % 2], part_max[:, :, 0])
                    last.then_inc(max_ready, 1)
                    dve.wait_ge(max_ready, PRIMED + NB * g + s + 1)
                    if plan.search[s]:
                        V.tensor_tensor(thr[:, s % 3], row_max[:, s % 2], guess[:, 0, plan.tile[s]], ALU.subtract).then_inc(thr_ready[0], 1)

                def better_guess(s, n):
                    m = SE * g + plan.search0[s]
                    dve.wait_ge(probed, PRIMED + 3 * R * m + R * n)
                    first, off = miss[:, 0], miss[:, n - 1]
                    step(V.tensor_scalar(off, sums[:, s % 2, n - 1], -0.5, AIM - plan.keys[s] / 2, ALU.mult, ALU.add))
                    step(V.tensor_tensor(upd[:, 1], off, guess[:, 1, plan.tile[s]], ALU.mult))
                    if n == 2:
                        V.tensor_tensor(upd[:, 2], off, off, ALU.mult)
                        V.tensor_tensor(upd[:, 3], first, first, ALU.mult)
                        step(V.tensor_tensor(upd[:, 4], first, off, ALU.mult))
                        step(V.scalar_tensor_tensor(upd[:, 4], upd[:, 4], -0.01, upd[:, 3], ALU.min, ALU.subtract))
                        step(V.reciprocal(upd[:, 0], upd[:, 4]))
                        step(V.scalar_tensor_tensor(upd[:, 3], upd[:, 3], -1.0, upd[:, 0], ALU.mult, ALU.mult))
                        step(V.scalar_tensor_tensor(upd[:, 1], upd[:, 2], NEAR * NEAR, upd[:, 1], ALU.is_gt, ALU.mult))
                        step(V.tensor_tensor(upd[:, 1], upd[:, 1], upd[:, 3], ALU.mult))
                    V.tensor_tensor(thr[:, s % 3], thr[:, s % 3], upd[:, 1], ALU.add).then_inc(thr_ready[n], 1)

                def candidates(s, r, between):
                    N = plan.keys[s]
                    w = gap[:, s % 3, r, 0:N]
                    if r == 0:
                        dve.wait_ge(thr_ready[2], PRIMED + SE * g + plan.search0[s] + 1)
                    sync()
                    put(V.scalar_tensor_tensor(near[:, 0:N], w, thr[:, s % 3, r:r + 1], w, ALU.is_le, ALU.mult))
                    between()
                    sync()
                    for p in range(PARTS):
                        last = V.max(cand[:, r, p], near[:, p * N // PARTS:(p + 1) * N // PARTS])
                    put(last)
                    between()

                def rounds():
                    sync()
                    pool = [cand[:, r].rearrange("p a b -> p (a b)") for r in range(R)]
                    for n in range(ROUNDS):
                        for r in range(R):
                            last = V.max(best[:, r, 8 * n:8 * n + 8], pool[r])
                        step(last)
                        if n < ROUNDS - 1:
                            for r in range(R):
                                last = V.match_replace(cand2[:, n, r], best[:, r, 8 * n:8 * n + 8], pool[r], -1.0)
                                pool[r] = cand2[:, n, r]
                            step(last)

                def settle(s):
                    m = SE * g + plan.search0[s]
                    c = cut[:, s % 2]
                    t = thr[:, s % 3]
                    wide = lambda ap: spread(ap.unsqueeze(2), [P, R, WINDOW])
                    step(V.tensor_tensor(hit[:], best[:], wide(t), ALU.is_equal))
                    step(V.tensor_reduce(small[:, 0], hit[:], AX, ALU.add))
                    dve.wait_ge(probed, PRIMED + 3 * R * m + 3 * R)
                    step(V.tensor_tensor(small[:, 1], small[:, 0], sums[:, s % 2, 2], ALU.add))
                    step(V.tensor_scalar(small[:, 0], small[:, 1], 0.5, plan.keys[s] / 2 - KEEP, ALU.mult, ALU.add))
                    step(V.tensor_tensor(hit[:], rank_sb[:], wide(small[:, 0]), ALU.is_equal))
                    step(V.tensor_tensor(hit[:], hit[:], best[:], ALU.mult))
                    V.tensor_scalar(small[:, 2], small[:, 0], -(WINDOW - 1) / 2, None, ALU.add)
                    step(V.tensor_reduce(c, hit[:], AX, ALU.add))
                    V.tensor_tensor(small[:, 5], small[:, 2], small[:, 2], ALU.mult)
                    step(V.tensor_reduce(small[:, 1], cand[:, :, :, 7], AX, ALU.max))
                    V.tensor_tensor(small[:, 3], small[:, 1], c, ALU.is_gt)
                    step(V.tensor_tensor(small[:, 4], small[:, 1], t, ALU.is_ge))
                    step(V.tensor_tensor(small[:, 3], small[:, 3], small[:, 4], ALU.max))
                    last = V.scalar_tensor_tensor(bad[:], small[:, 5], (WINDOW / 2) ** 2, small[:, 3], ALU.is_gt, ALU.max)
                    if plan.tile[s] == 1:
                        step(last)
                        step(V.tensor_scalar(c, c, floor_sb[:, 0:1], None, ALU.max))
                        last = V.tensor_scalar(bad[:], bad[:], floor_sb[:, 1:2], None, ALU.mult)
                    last.then_inc(bad_ready, 1)

                def check_flag(s):
                    m = SE * g + plan.search0[s]
                    dve.wait_ge(flag_ready, PRIMED + m + 1)
                    V.tensor_reduce(flag[:], ps_x[0:1, 0:R], AX, ALU.max).then_inc(flag_read, 1)
                    dve.wait_ge(flag_read, PRIMED + m + 1)
                    step(V.tensor_copy(flag_at[:], flag[:]))
                    found = dve.value_load(flag_at[0:1, 0:1])
                    with dve.If(found > 0):
                        bisect(s)

                def bisect(s):
                    N = plan.keys[s]
                    dve.sem_clear(fchain)
                    fstep = ordered(dve, fchain)
                    fstep(V.memset(f_bits[:], 0))
                    with dve.Fori(0, 31) as i:
                        dve.sem_clear(fchain)
                        fstep = ordered(dve, fchain)
                        bit = spread(bits_sb[:, bass.ds(i, 1)], [P, R])
                        fstep(V.tensor_tensor(f_try[:], f_bits[:], bit, ALU.bitwise_or))
                        for r in range(R):
                            fstep(V.tensor_scalar(near[:, 0:N], gap[:, s % 3, r, 0:N], f_try[:, r:r + 1].bitcast(F32), None,
                                                  ALU.is_lt, ALU.add, accum_out=f_count[:, r:r + 1]))
                        fstep(V.tensor_scalar(f_mask[:], f_count[:], KEEP - 0.5, -1.0, ALU.is_lt, ALU.mult))
                        fstep(V.tensor_tensor(f_mask[:], f_mask[:], bit, ALU.bitwise_and))
                        fstep(V.tensor_tensor(f_bits[:], f_bits[:], f_mask[:], ALU.bitwise_or))
                    dve.sem_clear(fchain)
                    fstep = ordered(dve, fchain)
                    fstep(V.tensor_copy(cut[:, s % 2], f_bits[:].bitcast(F32)))
                    if plan.tile[s] == 1:
                        fstep(V.tensor_scalar(cut[:, s % 2], cut[:, s % 2], floor_sb[:, 0:1], None, ALU.max))

                def keep(s, r):
                    N = plan.keys[s]
                    dve.wait_ge(exp_ready, PRIMED + R * NB * g + R * s + r + 1)
                    V.scalar_tensor_tensor(prob[:, s % 2, r, 0:N], gap[:, s % 3, r, 0:N], cut[:, s % 2, r:r + 1],
                                           prob[:, s % 2, r, 0:N], ALU.is_le, ALU.mult).then_inc(kept_ready, 1)

                def normalize(s):
                    dve.wait_ge(pv_done, PRIMED + BL * g + plan.block0[s + 1])
                    if s:
                        dve.wait_ge(ot_turned, PRIMED + NB * g + s)
                    o = ps_o[:, 0:R * (HD + 1)].rearrange("p (r d) -> p r d", r=R)
                    step(V.reciprocal(rden[:], o[:, :, HD]))
                    V.tensor_tensor(o_sb[:].rearrange("p (r d) -> p r d", r=R), o[:, :, 0:HD],
                                    spread(rden[:].unsqueeze(2), [P, R, HD]), ALU.mult).then_inc(out_ready, 1)

                dve.wait_ge(guess_in, PRIMED + 16 * g + 16)
                for piece in pieces(0):
                    read_scores(0, piece)
                first_guess(0)
                for k in range(NB + 3):
                    mine = 0 <= k - 1 < NB and plan.search[k - 1]
                    here = 0 <= k < NB and plan.search[k]
                    ahead = pieces(k + 1) if k + 1 < NB else []

                    def some(n):
                        for piece in ahead[:n]:
                            read_scores(k + 1, piece)
                        del ahead[:n]

                    if mine:
                        old = [k - 3] if k >= 3 else []

                        def between():
                            if old:
                                normalize(old.pop())
                            some(1)

                        for r in range(R):
                            candidates(k - 1, r, between)
                            if r == 2 and here:
                                better_guess(k, 1)
                        rounds()
                        some(8)
                    else:
                        if 0 <= k - 3 < NB:
                            normalize(k - 3)
                        some(8)
                        if here:
                            better_guess(k, 1)
                    if k + 1 < NB:
                        first_guess(k + 1)
                    if mine:
                        settle(k - 1)
                    if here:
                        better_guess(k, 2)
                    if mine:
                        check_flag(k - 1)
                        for r in range(R):
                            keep(k - 1, r)


def output_program(nc, x, wo, wf, bb, at_d, xt_d, zp_d, out):
    with ExitStack() as ctx:
        sb = lambda n, s, d=F32: ctx.enter_context(nc.sbuf_tensor(n, s, d))
        primed = []
        sem = semaphores(nc, ctx, primed)
        wo_sb = sb("wo_sb", [P, C, D])
        wf_sb = sb("wf_sb", [P, C, D])
        bb_sb = sb("bb_sb", [RANK + 1, D])
        at = sb("o_at", [P, 2, C, P])
        xt = sb("o_xt", [P, 2, C, P])
        zp = sb("o_zp", [RANK + 1, 2, P])
        xr = sb("o_xr", [P, 2, D])
        y = sb("o_y", [P, 2, D])
        ps = ctx.enter_context(nc.psum_tensor("o_ps", [P, 2, D], F32))
        weights_in = sem("o_weights_in")
        tile_in = [sem("o_tile_in0"), sem("o_tile_in1")]
        summed = sem("o_summed")
        done = sem("o_done")
        stored = [sem("o_stored0"), sem("o_stored1")]
        prime(nc, primed)
        block = ctx.enter_context(nc.Block("output"))

        @block.sync
        def _(sp):
            for dst, src in ((wf_sb, wf), (bb_sb, bb), (wo_sb, wo)):
                sp.dma_start(dst[:], src).then_inc(weights_in, 16)
            with sp.Fori(0, T // 2) as i:
                for h in range(2):
                    t = 2 * i + h
                    sp.wait_ge(done, PRIMED + 2 * i)
                    sp.dma_start(at[:, h], at_d[t]).then_inc(tile_in[h], 16)
                    sp.dma_start(xt[:, h], xt_d[t]).then_inc(tile_in[h], 16)
                    sp.dma_start(zp[:, h], zp_d[:, bass.ts(t, P)]).then_inc(tile_in[h], 16)
                    sp.dma_start(xr[:, h], x[t]).then_inc(tile_in[h], 16)

        @block.scalar
        def _(act):
            with act.Fori(0, T // 2) as i:
                for h in range(2):
                    act.wait_ge(done, PRIMED + 2 * i + h + 1)
                    act.dma_start(out[2 * i + h], y[:, h]).then_inc(stored[h], 16)
            for h in range(2):
                act.wait_ge(stored[h], PRIMED + 16 * (T // 2))

        @block.tensor
        def _(pe):
            pe.wait_ge(weights_in, PRIMED + 48)
            with pe.Fori(0, T // 2) as i:
                for h in range(2):
                    pe.wait_ge(tile_in[h], PRIMED + 64 * i + 64)
                    pe.wait_ge(done, PRIMED + 2 * i)
                    for j in range(2):
                        cols = bass.ts(j, 512)
                        for c in range(C):
                            pe.matmul(ps[:, h, cols], xt[:, h, c], wf_sb[:, c, cols], start=(c == 0), stop=False)
                        for c in range(C):
                            pe.matmul(ps[:, h, cols], at[:, h, c], wo_sb[:, c, cols], start=False, stop=False)
                        mm = pe.matmul(ps[:, h, cols], zp[:, h], bb_sb[:, cols], start=False, stop=True)
                    mm.then_inc(summed, 1)

        @block.vector
        def _(dve):
            with dve.Fori(0, T // 2) as i:
                for h in range(2):
                    dve.wait_ge(summed, PRIMED + 2 * i + h + 1)
                    dve.wait_ge(stored[h], PRIMED + 16 * i)
                    nc.vector.tensor_tensor(y[:, h], ps[:, h], xr[:, h], ALU.add).then_inc(done, 1)


def build(nc, a):
    with ExitStack() as ctx:
        dram = lambda n, s: nc.dram_tensor(n, s, F32).ap()
        xt_d = dram("xt_d", [T, P, C, P])
        vt_d = dram("vt_d", [T, P, G, HD + 1])
        zp_d = dram("zp_d", [RANK + 1, S])
        qk_d = dram("qk_d", [G, 2, P, S])
        stat_d = dram("stat_d", [G, P, 2, T * R])
        at_d = dram("at_d", [T, P, G, P])
        x = a["x"].rearrange("(t p) d -> t p d", p=P)
        with ExitStack() as early:
            z_keep = early.enter_context(nc.sbuf_tensor("z_keep", [RANK, S], F32))
            gate_in = early.enter_context(nc.sbuf_tensor("gate_in", [A, T, 2 * E], F32))
            tokens_program(nc, x, a["wv"], a["a_in"], a["w8"], a["b8"], a["lime_t"], a["ident"], xt_d, vt_d, z_keep, gate_in)
            router_program(nc, a["lime"], a["ident"], zp_d, z_keep, gate_in)
        heads_program(nc, a["wqk"], xt_d, a["cos"], a["sin"], a["rot_t"], a["ident"], a["block_mean"], a["head_sel"], a["zrow"], qk_d, stat_d)
        attention_program(nc, qk_d, vt_d, stat_d, at_d, a["ident"], a["ident_bf"], a["causal_bf"], a["bits"], a["ranks"], a["floors"])
        output_program(nc, x, a["wo"], a["wf"], a["bb"], at_d, xt_d, zp_d, a["out"].rearrange("(t p) d -> t p d", p=P))


def normal_tail(share):
    low, high = -10.0, 10.0
    for _ in range(60):
        z = (low + high) / 2
        if math.erfc(z / math.sqrt(2)) / 2 > share:
            low = z
        else:
            high = z
    return z


def as_bf16(table):
    upper = (np.ascontiguousarray(table, np.float32).view(np.uint32) >> 16).astype(np.uint16)
    return upper.view(np.int32)


def constants():
    f = np.float32
    inv = f(1) / np.power(f(10000), np.arange(0, HD, 2, dtype=f) / f(HD))
    angle = np.arange(S, dtype=f)[:, None] * inv
    lay = lambda t: np.ascontiguousarray(np.tile(np.concatenate([t, t], 1).T, (R, 1)))
    rot = np.zeros((P, P), f)
    for h in range(R):
        for d in range(HD // 2):
            rot[HD * h + d, HD * h + d + HD // 2] = -1
            rot[HD * h + d + HD // 2, HD * h + d] = 1
    same = np.kron(np.eye(R), np.ones((HD, HD)))
    zrow = np.zeros((3, S))
    for n in range(1, S + 1):
        if n < KEEP + WINDOW:
            zrow[1, n - 1] = -BIG
        else:
            z = normal_tail(AIM / n)
            zrow[0, n - 1] = z
            zrow[2, n - 1] = math.sqrt(2 * math.pi) * math.exp(z * z / 2) / n
    zrow = np.repeat(zrow.reshape(3, T, P).transpose(2, 0, 1)[..., None], R, -1).reshape(P, 3, T * R)
    row = np.arange(P)
    few = P + row + 1 < KEEP
    return {
        "ident": np.eye(P, dtype=f), "rot_t": np.ascontiguousarray(rot.T),
        "cos": lay(np.cos(angle)), "sin": lay(np.sin(angle)),
        "block_mean": (same * (SCALE * SCALE / S)).astype(f),
        "head_sel": np.kron(np.eye(R), np.ones((HD, 1))).astype(f),
        "zrow": zrow.astype(f),
        "ident_bf": as_bf16(np.eye(P)),
        "causal_bf": as_bf16(np.where(row[:, None] < row[None, :], MASKED, 0)),
        "bits": np.tile((1 << np.arange(30, -1, -1)).astype(np.int32), (P, 1)),
        "ranks": np.tile(np.arange(WINDOW, dtype=f), (P, R, 1)),
        "floors": np.stack([np.where(few, BIG, 0), np.where(few, 0, 1)], 1).astype(f),
    }


def kernel(**inputs):
    import concourse.bacc as bacc
    from concourse.bass_utils import run_bass_kernel_spmd

    n = {k: np.asarray(v) for k, v in inputs.items()}
    by_chunk = lambda w: np.ascontiguousarray(w.T.reshape(C, P, -1).transpose(1, 0, 2))
    wq = by_chunk(n["L0_attn_Wq"]).reshape(P, C, G, P)
    wk = by_chunk(n["L0_attn_Wk"]).reshape(P, C, G, 1, HD)
    wk = np.broadcast_to(wk, (P, C, G, R, HD)).reshape(P, C, G, P)
    arrays = {
        "x": n["L0_attn_hidden_states"].reshape(S, D),
        "wqk": np.ascontiguousarray(np.concatenate([wk, wq], -1).transpose(2, 0, 1, 3)),
        "wv": by_chunk(n["L0_attn_Wv"]),
        "wo": by_chunk(n["L0_attn_Wo"]),
        "wf": by_chunk(n["L0_ffn_W"]),
        "w8": by_chunk(n["L0_ffn_W"][:E]),
        "b8": np.ascontiguousarray(n["L0_ffn_b"][None, :E]),
        "a_in": np.ascontiguousarray(n["L0_ffn_A"].reshape(C, P, RANK).transpose(1, 0, 2)),
        "bb": np.concatenate([n["L0_ffn_Bmat"], n["L0_ffn_b"][None]], 0),
        "lime": n["L0_ffn_LiMEs"],
        "lime_t": np.ascontiguousarray(n["L0_ffn_LiMEs"].T),
        **constants(),
    }
    arrays = {k: np.ascontiguousarray(v) for k, v in arrays.items()}
    nc = bacc.Bacc("TRN2", target_bir_lowering=False, num_devices=1)
    aps = {k: nc.dram_tensor(k, v.shape, mybir.dt.from_np(v.dtype), kind="ExternalInput").ap() for k, v in arrays.items()}
    aps["out"] = nc.dram_tensor("out", (S, D), F32, kind="ExternalOutput").ap()
    build(nc, aps)
    r = run_bass_kernel_spmd(nc, [arrays], core_ids=[0])
    return r.results[0]["out"].reshape(1, S, D)
```

```python
import math
from contextlib import ExitStack

import numpy as np

import concourse.bass as bass
from concourse import mybir

ALU = mybir.AluOpType
ACT = mybir.ActivationFunctionType
F32 = mybir.dt.float32
I32 = mybir.dt.int32
BF16 = mybir.dt.bfloat16
AX = mybir.AxisListType.X
RMAX = bass.bass_isa.ReduceOp.max

P = 128
S = 2048
D = 1024
C = D // P
T = S // P
HD = 32
G = 8
R = 4
RANK = 32
E = 8
A = P // 2
KEEP = max(min(S, 128), S - int(S * 0.9))
SCALE = float(np.float32(1) / np.float32(np.sqrt(HD)))
LN_EPS = 1e-5
BIG = 1e20
MASKED = -1e30

ROUNDS = 3
WINDOW = 8 * ROUNDS
AIM = KEEP + 8.5
NEAR = 4.0
PARTS = 11
CHUNK = 1024
MIDDLE = 512


PRIMED = 1


def semaphores(nc, ctx, primed):
    def sem(name):
        primed.append(ctx.enter_context(nc.semaphore(name)))
        return primed[-1]
    return sem


def prime(nc, sems):
    with nc.Block() as block:
        @block.sync
        def _(sp):
            for s in sems:
                sp.sem_inc(s, PRIMED)


def batches():
    return [0, 3, 5, 7, 9, 11, 13, 15, 14, 12, 10, 8, 6, 4, 2, 1]


def ordered(engine, sem):
    count = [0]

    def step(instruction):
        count[0] += 1
        instruction.then_inc(sem, 1)
        engine.wait_ge(sem, count[0])
    return step


def paced(engine, sem):
    count = [0]

    def put(instruction):
        count[0] += 1
        instruction.then_inc(sem, 1)

    def sync():
        engine.wait_ge(sem, count[0])
    return put, sync


def two_before(i, h):
    return 0 if isinstance(i, int) and i == 0 else 2 * i + h - 1


def spread(ap, shape):
    return ap.broadcast_to(list(shape))


def tokens_program(nc, x, wv, a_in, w8, b8, lime_t, ident, xt_d, vt_d, z_keep, gate_in):
    with ExitStack() as ctx:
        sb = lambda n, s, d=F32: ctx.enter_context(nc.sbuf_tensor(n, s, d))
        primed = []
        sem = semaphores(nc, ctx, primed)
        pb = lambda n, s: ctx.enter_context(nc.psum_tensor(n, s, F32))
        wv_sb = sb("wv_sb", [P, C, G * HD])
        a_sb = sb("a_sb", [P, C, RANK])
        w8_sb = sb("w8_sb", [P, C, E])
        b8_sb = sb("b8_sb", [1, E])
        lt_sb = sb("lt_sb", [RANK, E])
        id_sb = sb("id_sb", [P, P])
        one_row = sb("one_row", [1, A])
        xin = sb("xin", [P, 2, D])
        xn = sb("xn", [P, 2, D])
        xt = sb("xt", [P, 2, C, P])
        vt = sb("vt", [P, 2, G, HD])
        zt = sb("zt", [RANK, 2, P])
        stats = sb("stats", [P, 2, 6])
        mv = sb("mv", [P, 2])
        sd = sb("sd", [P, 1])
        rs = sb("rs", [P, 4])
        ps_t = pb("ps_t", [P, 2, C * P])
        ps_v = pb("ps_v", [P, 2, 512])
        ps_z = pb("ps_z", [P, 512])
        ps_g = pb("ps_g", [P, 512])

        weights_in = sem("weights_in")
        x_in = [sem("x_in0"), sem("x_in1")]
        var_ready = sem("var_ready")
        sd_ready = sem("sd_ready")
        xn_ready = sem("xn_ready")
        turned = sem("turned")
        xt_ready = sem("xt_ready")
        v_ready = sem("v_ready")
        z_ready = sem("z_ready")
        zt_ready = sem("zt_ready")
        gate_ready = sem("gate_ready")
        v_read = sem("v_read")
        gate_read = sem("gate_read")
        ones_ready = sem("ones_ready")
        stored = [sem("stored0"), sem("stored1")]
        chain = ctx.enter_context(nc.semaphore("chain"))
        prime(nc, primed)
        block = ctx.enter_context(nc.Block("tokens"))

        @block.sync
        def _(sp):
            for dst, src in ((id_sb, ident), (wv_sb, wv), (a_sb, a_in), (w8_sb, w8), (b8_sb, b8), (lt_sb, lime_t)):
                sp.dma_start(dst[:], src).then_inc(weights_in, 16)
            with sp.Fori(0, T // 2) as i:
                for h in range(2):
                    sp.wait_ge(xn_ready, PRIMED + 2 * i)
                    sp.dma_start(xin[:, h], x[2 * i + h]).then_inc(x_in[h], 16)
            for h in range(2):
                sp.wait_ge(stored[h], PRIMED + 32 * (T // 2))

        @block.gpsimd
        def _(pool):
            nc.gpsimd.memset(one_row[:], 1.0).then_inc(ones_ready, 1)

        @block.vector
        def _(dve):
            def normalize(i, h, step):
                t = 2 * i + h
                dve.wait_ge(xn_ready, PRIMED + t)
                dve.wait_ge(x_in[h], PRIMED + 16 * i + 16)
                nc.vector.bn_stats(stats[:, 0], xin[:, h, 0:D // 2])
                step(nc.vector.bn_stats(stats[:, 1], xin[:, h, D // 2:D]))
                step(nc.vector.bn_aggr(mv[:], stats[:]))
                nc.vector.tensor_scalar(mv[:, 1:2], mv[:, 1:2], LN_EPS, None, ALU.add).then_inc(var_ready, 1)
                dve.wait_ge(sd_ready, PRIMED + t + 1)
                step(nc.vector.reciprocal(rs[:, 0:1], sd[:]))
                step(nc.vector.scalar_tensor_tensor(rs[:, 1:2], rs[:, 0:1], rs[:, 0:1], mv[:, 1:2], ALU.mult, ALU.mult))
                step(nc.vector.tensor_scalar(rs[:, 2:3], rs[:, 1:2], -0.5, 1.5, ALU.mult, ALU.add))
                step(nc.vector.tensor_tensor(rs[:, 3:4], rs[:, 0:1], rs[:, 2:3], ALU.mult))
                dve.wait_ge(turned, PRIMED + two_before(i, h))
                nc.vector.tensor_scalar(xn[:, h], xin[:, h], mv[:, 0:1], rs[:, 3:4], ALU.subtract, ALU.mult).then_inc(xn_ready, 1)

            def read_products(i, h):
                t = 2 * i + h
                dve.wait_ge(v_ready, PRIMED + t + 1)
                dve.wait_ge(stored[h], PRIMED + 32 * i)
                nc.vector.tensor_copy(vt[:, h], ps_v[:, h, 0:G * HD].rearrange("p (g d) -> p g d", g=G)).then_inc(v_read, 1)
                dve.wait_ge(gate_ready, PRIMED + t + 1)
                nc.vector.tensor_copy(gate_in[:, bass.ds(t, 1)], ps_g[0:A, 0:2 * E]).then_inc(gate_read, 1)

            normalize(0, 0, ordered(dve, chain))
            with dve.Fori(0, T // 2 - 1) as i:
                dve.sem_clear(chain)
                step = ordered(dve, chain)
                normalize(i, 1, step)
                read_products(i, 0)
                normalize(i + 1, 0, step)
                read_products(i, 1)
            dve.sem_clear(chain)
            normalize(T // 2 - 1, 1, ordered(dve, chain))
            for h in range(2):
                read_products(T // 2 - 1, h)

        @block.scalar
        def _(act):
            def root(i, h):
                act.wait_ge(var_ready, PRIMED + 2 * i + h + 1)
                act.wait_ge(xn_ready, PRIMED + 2 * i + h)
                nc.scalar.activation(sd[:], mv[:, 1:2], ACT.Sqrt).then_inc(sd_ready, 1)

            def copy_turned(i, h):
                act.wait_ge(turned, PRIMED + 2 * i + h + 1)
                act.wait_ge(stored[h], PRIMED + 32 * i)
                act.wait_ge(gate_ready, PRIMED + two_before(i, h))
                nc.scalar.activation(xt[:, h], ps_t[:, h].rearrange("p (c k) -> p c k", c=C), ACT.Copy).then_inc(xt_ready, 1)

            def copy_z(i, h):
                t = 2 * i + h
                act.wait_ge(z_ready, PRIMED + t + 1)
                nc.scalar.activation(zt[:, h], ps_z[0:RANK, 0:P], ACT.Copy).then_inc(zt_ready, 1)
                nc.scalar.activation(z_keep[:, bass.ts(t, P)], ps_z[0:RANK, 0:P], ACT.Copy).then_inc(zt_ready, 1)

            def store(i, h):
                t = 2 * i + h
                act.wait_ge(xt_ready, PRIMED + t + 1)
                act.dma_start(xt_d[t], xt[:, h]).then_inc(stored[h], 16)
                act.wait_ge(v_read, PRIMED + t + 1)
                act.dma_start(vt_d[t], vt[:, h]).then_inc(stored[h], 16)

            root(0, 0)
            copy_turned(0, 0)
            with act.Fori(0, T // 2 - 1) as i:
                for h in range(2):
                    root(i + h, 1 - h)
                    copy_turned(i + h, 1 - h)
                    copy_z(i, h)
                    store(i, h)
            root(T // 2 - 1, 1)
            copy_turned(T // 2 - 1, 1)
            for h in range(2):
                copy_z(T // 2 - 1, h)
                store(T // 2 - 1, h)

        @block.tensor
        def _(pe):
            def turn(i, h):
                t = 2 * i + h
                pe.wait_ge(xn_ready, PRIMED + t + 1)
                pe.wait_ge(xt_ready, PRIMED + two_before(i, h))
                for c in range(C):
                    mm = pe.transpose(ps_t[:, h, bass.ts(c, P)], xn[:, h, bass.ts(c, P)], id_sb[:])
                mm.then_inc(turned, 1)

            def products(i, h):
                t = 2 * i + h
                pe.wait_ge(xt_ready, PRIMED + t + 1)
                pe.wait_ge(v_read, PRIMED + 2 * i)
                for c in range(C):
                    mm = pe.matmul(ps_v[:, h, 0:G * HD], xt[:, h, c], wv_sb[:, c], start=(c == 0), stop=(c == C - 1))
                mm.then_inc(v_ready, 1)
                pe.wait_ge(zt_ready, PRIMED + 2 * t)
                for c in range(C):
                    mm = pe.matmul(ps_z[0:RANK, 0:P], a_sb[:, c], xt[:, h, c], start=(c == 0), stop=(c == C - 1))
                mm.then_inc(z_ready, 1)
                pe.wait_ge(gate_read, PRIMED + t)
                for c in range(C):
                    pe.matmul(ps_g[0:A, 0:E], xt[:, h, c, 1:P:2], w8_sb[:, c], start=(c == 0), stop=False, skip_group_check=True)
                pe.matmul(ps_g[0:A, 0:E], one_row[:], b8_sb[:], start=False, stop=True, skip_group_check=True)
                pe.wait_ge(zt_ready, PRIMED + 2 * t + 2)
                pe.matmul(ps_g[0:A, E:2 * E], zt[:, h, 1:P:2], lt_sb[:], start=False, stop=True, skip_group_check=True).then_inc(gate_ready, 1)

            pe.wait_ge(weights_in, PRIMED + 16 * 6)
            pe.wait_ge(ones_ready, PRIMED + 1)
            turn(0, 0)
            with pe.Fori(0, T // 2 - 1) as i:
                for h in range(2):
                    turn(i + h, 1 - h)
                    products(i, h)
            turn(T // 2 - 1, 1)
            for h in range(2):
                products(T // 2 - 1, h)


def router_program(nc, lime, ident, zp_d, z_keep, gate_in):
    with ExitStack() as ctx:
        sb = lambda n, s, d=F32: ctx.enter_context(nc.sbuf_tensor(n, s, d))
        primed = []
        sem = semaphores(nc, ctx, primed)
        lm_sb = sb("lm_sb", [E, RANK])
        id_sb = sb("rt_id_sb", [P, P])
        peak = sb("peak", [A, 2])
        peak_all = sb("peak_all", [A, 2])
        half = sb("half", [A, 2])
        lg = sb("lg", [A, T, E])
        lg2 = sb("lg2", [A, T, E])
        sig = sb("sig", [A, T, E])
        row = sb("row", [A, T])
        row2 = sb("row2", [A, T])
        top = sb("top", [A, T, 8])
        wt = sb("wt", [E, T * A])
        zp = sb("zp", [RANK + 1, S])
        ps_w = ctx.enter_context(nc.psum_tensor("ps_w", [P, 2, 512], F32))
        ps_m = ctx.enter_context(nc.psum_tensor("ps_m", [P, 2, 512], F32))
        loaded = sem("rt_loaded")
        peak_ready = sem("peak_ready")
        peak_shared = sem("peak_shared")
        logits_ready = sem("logits_ready")
        exp_ready = sem("rt_exp_ready")
        probs_ready = sem("rt_probs_ready")
        sig_ready = sem("sig_ready")
        weights_ready = sem("weights_ready")
        turned = sem("rt_turned")
        wt_ready = sem("wt_ready")
        mix_ready = sem("mix_ready")
        zp_ready = sem("zp_ready")
        stored = sem("rt_stored")
        chain = ctx.enter_context(nc.semaphore("rt_chain"))
        prime(nc, primed)
        block = ctx.enter_context(nc.Block("router"))
        per_row = lambda ap: spread(ap[:].unsqueeze(2), [A, T, E])

        @block.sync
        def _(sp):
            sp.dma_start(lm_sb[:], lime).then_inc(loaded, 16)
            sp.dma_start(id_sb[:], ident).then_inc(loaded, 16)
            sp.wait_ge(zp_ready, PRIMED + 1)
            sp.dma_start(zp_d, zp[:]).then_inc(stored, 16)
            sp.wait_ge(stored, PRIMED + 16)

        @block.gpsimd
        def _(pool):
            pool.wait_ge(peak_ready, PRIMED + 1)
            nc.gpsimd.partition_all_reduce(peak_all[:], peak[:], A, RMAX).then_inc(peak_shared, 1)

        @block.scalar
        def _(act):
            act.wait_ge(logits_ready, PRIMED + 1)
            nc.scalar.activation(lg[:], lg2[:], ACT.Exp).then_inc(exp_ready, 1)
            act.wait_ge(probs_ready, PRIMED + 1)
            nc.scalar.activation(sig[:], lg2[:], ACT.Exp, scale=-2.0).then_inc(sig_ready, 1)

        @block.tensor
        def _(pe):
            pe.wait_ge(loaded, PRIMED + 32)
            pe.wait_ge(weights_ready, PRIMED + 1)
            for t in range(T):
                mm = pe.transpose(ps_w[0:E, t // 8, bass.ts(t % 8, A)], lg[:, t], id_sb[0:A, 0:A])
            mm.then_inc(turned, 1)
            pe.wait_ge(wt_ready, PRIMED + 1)
            for j in range(2):
                mm = pe.matmul(ps_m[0:RANK, j], lm_sb[:], wt[:, bass.ts(j, 512)], start=True, stop=True)
            mm.then_inc(mix_ready, 1)

        @block.vector
        def _(dve):
            step = ordered(dve, chain)
            V = nc.vector
            step(V.memset(zp[:], 1.0))
            for n in range(2):
                part = gate_in[:, :, bass.ts(n, E)]
                step(V.scalar_tensor_tensor(lg[:], part, -1.0, part, ALU.mult, ALU.max))
                last = V.tensor_reduce(peak[:, n:n + 1], lg[:].rearrange("p t e -> p (t e)"), AX, ALU.max)
                if n == 0:
                    step(last)
                else:
                    last.then_inc(peak_ready, 1)
            dve.wait_ge(peak_shared, PRIMED + 1)
            step(V.tensor_scalar(half[:], peak_all[:], 1e-6, None, ALU.max))
            step(V.reciprocal(peak[:], half[:]))
            step(V.tensor_scalar(half[:], peak[:], 0.5, None, ALU.mult))
            step(V.tensor_scalar(lg[:], gate_in[:, :, E:2 * E], half[:, 1:2], None, ALU.mult))
            step(V.scalar_tensor_tensor(lg[:], gate_in[:, :, 0:E], half[:, 0:1], lg[:], ALU.mult, ALU.add))
            step(V.tensor_reduce(row[:], lg[:], AX, ALU.max))
            V.tensor_tensor(lg2[:], lg[:], per_row(row), ALU.subtract).then_inc(logits_ready, 1)
            dve.wait_ge(exp_ready, PRIMED + 1)
            step(V.tensor_reduce(row[:], lg[:], AX, ALU.add))
            step(V.reciprocal(row2[:], row[:]))
            step(V.tensor_tensor(lg[:], lg[:], per_row(row2), ALU.mult))
            for t in range(T):
                last = V.max(top[:, t], lg[:, t])
            step(last)
            V.tensor_tensor(lg2[:], lg[:], spread(top[:, :, 1:2], [A, T, E]), ALU.subtract).then_inc(probs_ready, 1)
            dve.wait_ge(sig_ready, PRIMED + 1)
            step(V.tensor_scalar(sig[:], sig[:], 1.0, None, ALU.add))
            step(V.reciprocal(lg2[:], sig[:]))
            step(V.tensor_tensor(lg2[:], lg2[:], lg[:], ALU.mult))
            step(V.tensor_reduce(row[:], lg2[:], AX, ALU.add))
            step(V.tensor_scalar(row[:], row[:], 1e-9, None, ALU.add))
            step(V.reciprocal(row2[:], row[:]))
            V.tensor_tensor(lg[:], lg2[:], per_row(row2), ALU.mult).then_inc(weights_ready, 1)
            dve.wait_ge(turned, PRIMED + 1)
            nc.vector.tensor_copy(wt[:].rearrange("e (j n) -> e j n", j=2), ps_w[0:E]).then_inc(wt_ready, 1)
            dve.wait_ge(mix_ready, PRIMED + 1)
            V.scalar_tensor_tensor(
                zp[0:RANK].rearrange("r (a n) -> r a n", n=2), z_keep[:].rearrange("r (a n) -> r a n", n=2), 0.5,
                spread(ps_m[0:RANK].rearrange("r j n -> r (j n)").unsqueeze(2), [RANK, S // 2, 2]),
                ALU.mult, ALU.mult).then_inc(zp_ready, 1)


def heads_program(nc, wqk, xt_d, cos, sin, rot_t, repeat, ident, block_mean, head_sel, zrow, qk_d, stat_d):
    with ExitStack() as ctx:
        sb = lambda n, s, d=F32: ctx.enter_context(nc.sbuf_tensor(n, s, d))
        primed = []
        sem = semaphores(nc, ctx, primed)
        pb = lambda n, s: ctx.enter_context(nc.psum_tensor(n, s, F32))
        xt = sb("h_xt", [P, T, C, P])
        w_sb = sb("w_sb", [P, 2, C, 2 * P])
        cos_sb = sb("cos_sb", [P, S])
        sin_sb = sb("sin_sb", [P, S])
        rot_sb = sb("rot_sb", [P, P])
        rep_sb = sb("rep_sb", [P, P])
        k_by_chunk = sb("k_by_chunk", [P, 512])
        id_sb = sb("h_id_sb", [P, P])
        bm_sb = sb("bm_sb", [P, P])
        hs_sb = sb("hs_sb", [P, R])
        zr_sb = sb("zr_sb", [P, 3, T * R])
        raw = sb("raw", [P, 2, 512])
        tmp = sb("tmp", [P, 2, 512])
        qk = sb("qk", [P, 2, S])
        krow = sb("krow", [P, 2, P])
        cb = sb("cb", [P, P])
        km = sb("km", [P, 1])
        kmb = sb("kmb", [P, R])
        prod = sb("prod", [P, S])
        stat = sb("stat", [P, 2, T * R])
        sg = sb("sg", [P, 4, T * R])
        ps_p = pb("ps_p", [P, 2, 512])
        ps_r = pb("ps_r", [P, 2, 512])
        ps_k = pb("ps_k", [P, 2, 512])
        ps_c = pb("ps_c", [P, 512])
        ps_s = pb("ps_s", [P, 512])

        consts_in = sem("h_consts_in")
        x_in = [sem(f"h_x_in{n}") for n in range(4)]
        w_in = [sem("w_in0"), sem("w_in1")]
        proj_ready = sem("proj_ready")
        k_proj_ready = sem("k_proj_ready")
        k_copied = sem("k_copied")
        raw_ready = sem("raw_ready")
        rot_ready = sem("rot_ready")
        part_ready = sem("part_ready")
        krow_turned = sem("krow_turned")
        krow_ready = sem("krow_ready")
        krow_used = sem("krow_used")
        moments_used = sem("moments_used")
        moment_prod = sem("moment_prod")
        prod_ready = sem("prod_ready")
        square_ready = sem("square_ready")
        var_ready = sem("h_var_ready")
        dev_ready = sem("dev_ready")
        stat_ready = sem("stat_ready")
        stored = sem("h_stored")
        chain = ctx.enter_context(nc.semaphore("h_chain"))
        prime(nc, primed)
        block = ctx.enter_context(nc.Block("heads"))
        UNITS = 8

        @block.sync
        def _(sp):
            with sp.Fori(0, G // 2) as i:
                for h in range(2):
                    g = 2 * i + h
                    sp.wait_ge(proj_ready, PRIMED + 2 * UNITS * i)
                    sp.dma_start(w_sb[:, h], wqk[g]).then_inc(w_in[h], 16)
                for h in range(2):
                    g = 2 * i + h
                    sp.wait_ge(part_ready, PRIMED + UNITS * g + 4)
                    sp.dma_start(qk_d[g, 0], qk[:, 0]).then_inc(stored, 16)
                    sp.wait_ge(part_ready, PRIMED + UNITS * g + 8)
                    sp.dma_start(qk_d[g, 1], qk[:, 1]).then_inc(stored, 16)
                    sp.wait_ge(stat_ready, PRIMED + g + 1)
                    sp.dma_start(stat_d[g], stat[:]).then_inc(stored, 16)
            sp.wait_ge(stored, PRIMED + 48 * G)

        @block.tensor
        def _(pe):
            with pe.Fori(0, G // 2) as i:
                for h in range(2):
                    g = 2 * i + h
                    pe.wait_ge(w_in[h], PRIMED + 16 * i + 16)

                    def project_k():
                        pe.wait_ge(moments_used, PRIMED + g)
                        for j in range(4):
                            pe.wait_ge(x_in[j], PRIMED + 16)
                        for c in range(C):
                            for j in range(4):
                                mm = pe.matmul(ps_c[HD * j:HD * (j + 1)], w_sb[:, h, c, 0:HD], xt[:, 4 * j:4 * j + 4, c],
                                               start=(c == 0), stop=(c == C - 1), skip_group_check=True)
                        mm.then_inc(k_proj_ready, 1)
                        pe.wait_ge(consts_in, PRIMED + 16 * 8)
                        pe.wait_ge(k_copied, PRIMED + g + 1)

                    def project(u):
                        which, j = u // 4, u % 4
                        if u < 2:
                            pe.wait_ge(raw_ready, PRIMED + UNITS * g)
                        else:
                            pe.wait_ge(raw_ready, PRIMED + UNITS * g + u - 1)
                        if which == 0:
                            rows = slice(HD * j, HD * (j + 1))
                            mm = pe.matmul(ps_p[:, u % 2], rep_sb[rows], k_by_chunk[rows], start=True, stop=True)
                        else:
                            for c in range(C):
                                mm = pe.matmul(ps_p[:, u % 2], w_sb[:, h, c, bass.ts(which, P)],
                                               xt[:, 4 * j:4 * j + 4, c], start=(c == 0), stop=(c == C - 1))
                        mm.then_inc(proj_ready, 1)

                    def turn(u):
                        pe.wait_ge(consts_in, PRIMED + 16 * 8)
                        pe.wait_ge(raw_ready, PRIMED + UNITS * g + u + 1)
                        if u < 2:
                            pe.wait_ge(part_ready, PRIMED + UNITS * g)
                        else:
                            pe.wait_ge(part_ready, PRIMED + UNITS * g + u - 1)
                        pe.matmul(ps_r[:, u % 2], rot_sb[:], raw[:, u % 2], start=True, stop=True).then_inc(rot_ready, 1)

                    def k_rows(u):
                        pe.wait_ge(part_ready, PRIMED + UNITS * g + u + 1)
                        for n in range(4 * u, 4 * u + 4):
                            if n >= 2:
                                pe.wait_ge(krow_ready, PRIMED + T * g + n - 1)
                            else:
                                pe.wait_ge(krow_ready, PRIMED + T * g)
                            pe.transpose(ps_k[:, n % 2, 0:P], qk[:, 0, bass.ts(n, P)], id_sb[:]).then_inc(krow_turned, 1)
                            if n > 0:
                                moments(n - 1)

                    def moments(n):
                        pe.wait_ge(krow_ready, PRIMED + T * g + n + 1)
                        if n == 0:
                            pe.wait_ge(moments_used, PRIMED + g)
                        pe.matmul(ps_c[:, 0:P], krow[:, n % 2], krow[:, n % 2], start=(n == 0), stop=(n == T - 1)).then_inc(krow_used, 1)

                    project_k()
                    for u in range(UNITS):
                        project(u)
                        if u == 6:
                            moments(T - 1)
                        if u:
                            turn(u - 1)
                        if 2 <= u < 6:
                            k_rows(u - 2)
                    turn(UNITS - 1)
                    pe.wait_ge(moments_used, PRIMED + g + 1)
                    for j in range(4):
                        pe.wait_ge(part_ready, PRIMED + UNITS * g + 4 + j + 1)
                        pe.wait_ge(raw_ready, PRIMED + UNITS * g + UNITS)
                        if j >= 2:
                            pe.wait_ge(prod_ready, PRIMED + 4 * g + j - 1)
                        pe.matmul(ps_p[:, j % 2], cb[:], qk[:, 1, bass.ts(j, 512)], start=True, stop=True).then_inc(moment_prod, 1)
                    pe.wait_ge(prod_ready, PRIMED + 4 * g + 4)
                    pe.wait_ge(stat_ready, PRIMED + g)
                    for t in range(T):
                        pe.matmul(ps_s[:, bass.ts(t, R)], prod[:, bass.ts(t, P)], hs_sb[:], start=(t == 0), stop=True, skip_group_check=True)
                        mm = pe.matmul(ps_s[:, bass.ds(T * R + t * R, R)], qk[:, 1, bass.ts(t, P)], kmb[:], start=False, stop=True, skip_group_check=True)
                    mm.then_inc(square_ready, 1)

        @block.scalar
        def _(act):
            for n in range(4):
                if n == 1:
                    act.wait_ge(x_in[0], PRIMED + 16)
                    for dst, src in ((rep_sb, repeat), (rot_sb, rot_t), (cos_sb, cos), (sin_sb, sin), (id_sb, ident), (bm_sb, block_mean),
                                     (hs_sb, head_sel), (zr_sb, zrow)):
                        act.dma_start(dst[:], src).then_inc(consts_in, 16)
                act.dma_start(xt[:, 4 * n:4 * n + 4], xt_d[4 * n:4 * n + 4].rearrange("t p c k -> p t c k")).then_inc(x_in[n], 16)
            with act.Fori(0, G) as g:
                def copy_raw(u):
                    act.wait_ge(proj_ready, PRIMED + UNITS * g + u + 1)
                    act.wait_ge(part_ready, PRIMED + UNITS * g + u - 1) if u >= 2 else act.wait_ge(part_ready, PRIMED + UNITS * g)
                    nc.scalar.activation(raw[:, u % 2], ps_p[:, u % 2], ACT.Copy).then_inc(raw_ready, 1)

                def copy_rows(u):
                    for n in range(4 * u, 4 * u + 4):
                        act.wait_ge(krow_turned, PRIMED + T * g + n + 1)
                        act.wait_ge(krow_used, PRIMED + T * g + n - 1) if n >= 2 else act.wait_ge(krow_used, PRIMED + T * g)
                        nc.scalar.activation(krow[:, n % 2], ps_k[:, n % 2, 0:P], ACT.Copy).then_inc(krow_ready, 1)

                act.wait_ge(k_proj_ready, PRIMED + g + 1)
                nc.scalar.activation(k_by_chunk[:], ps_c[:], ACT.Copy).then_inc(k_copied, 1)
                for u in range(UNITS):
                    if u == 0:
                        act.wait_ge(prod_ready, PRIMED + 4 * g)
                    copy_raw(u)
                    if 2 <= u < 6:
                        copy_rows(u - 2)
                act.wait_ge(var_ready, PRIMED + g + 1)
                nc.scalar.activation(sg[:, 2], sg[:, 1], ACT.Sqrt).then_inc(dev_ready, 1)

        @block.vector
        def _(dve):
            V = nc.vector
            dve.wait_ge(consts_in, PRIMED + 16 * 8)
            with dve.Fori(0, G) as g:
                dve.sem_clear(chain)
                step = ordered(dve, chain)
                dve.wait_ge(stored, PRIMED + 48 * g)
                for u in range(UNITS):
                    which, j = u // 4, u % 4
                    cols = bass.ts(j, 512)
                    dve.wait_ge(raw_ready, PRIMED + UNITS * g + u + 1)
                    V.tensor_tensor(tmp[:, 0], raw[:, u % 2], cos_sb[:, cols], ALU.mult)
                    dve.wait_ge(rot_ready, PRIMED + UNITS * g + u + 1)
                    step(V.tensor_tensor(tmp[:, 1], ps_r[:, u % 2], sin_sb[:, cols], ALU.mult))
                    V.tensor_tensor(qk[:, which, cols], tmp[:, 0], tmp[:, 1], ALU.add).then_inc(part_ready, 1)
                    dve.wait_ge(part_ready, PRIMED + UNITS * g + u + 1)
                    if u == 3:
                        step(V.tensor_reduce(km[:], qk[:, 0], AX, ALU.add))
                        step(V.tensor_scalar(kmb[:], hs_sb[:], km[:, 0:1], SCALE / S, ALU.mult, ALU.mult))
                    if u == 6:
                        dve.wait_ge(krow_used, PRIMED + T * g + T)
                        V.tensor_tensor(cb[:], ps_c[:, 0:P], bm_sb[:], ALU.mult).then_inc(moments_used, 1)
                for j in range(4):
                    dve.wait_ge(moment_prod, PRIMED + 4 * g + j + 1)
                    V.tensor_tensor(prod[:, bass.ts(j, 512)], ps_p[:, j % 2], qk[:, 1, bass.ts(j, 512)], ALU.mult).then_inc(prod_ready, 1)
                dve.wait_ge(square_ready, PRIMED + g + 1)
                n = T * R
                step(V.tensor_copy(sg[:, 0], ps_s[:, n:2 * n]))
                step(V.tensor_tensor(sg[:, 3], sg[:, 0], sg[:, 0], ALU.mult))
                step(V.tensor_tensor(sg[:, 1], ps_s[:, 0:n], sg[:, 3], ALU.subtract))
                V.tensor_scalar(sg[:, 1], sg[:, 1], 0.0, None, ALU.max).then_inc(var_ready, 1)
                dve.wait_ge(dev_ready, PRIMED + g + 1)
                step(V.tensor_tensor(stat[:, 0], sg[:, 2], zr_sb[:, 0], ALU.mult))
                step(V.tensor_tensor(stat[:, 0], stat[:, 0], sg[:, 0], ALU.add))
                step(V.tensor_tensor(stat[:, 0], stat[:, 0], zr_sb[:, 1], ALU.add))
                V.tensor_tensor(stat[:, 1], sg[:, 2], zr_sb[:, 2], ALU.mult).then_inc(stat_ready, 1)
                dve.wait_ge(stat_ready, PRIMED + g + 1)


class Plan:

    def __init__(self):
        self.tile = batches()
        self.keys = [P * (b + 1) for b in self.tile]
        self.chunks = [R * -(-n // CHUNK) for n in self.keys]
        before = lambda xs: [sum(xs[:i]) for i in range(len(xs) + 1)]
        self.chunk0 = before(self.chunks)
        self.block0 = before([b + 1 for b in self.tile])
        self.search = [int(n > KEEP) for n in self.keys]
        self.search0 = before(self.search)
        self.n = len(self.tile)


def attention_program(nc, qk_d, vt_d, stat_d, at_d, ident, ident_bf, causal_bf, bits, ranks, floors, head_rows_d):
    plan = Plan()
    NB = plan.n
    CH, BL, SE = plan.chunk0[NB], plan.block0[NB], plan.search0[NB]
    assert CH % 2 == 0 and BL % 2 == 0
    with ExitStack() as ctx:
        sb = lambda n, s, d=F32: ctx.enter_context(nc.sbuf_tensor(n, s, d))
        primed = []
        sem = semaphores(nc, ctx, primed)
        pb = lambda n, s: ctx.enter_context(nc.psum_tensor(n, s, F32))
        qt = sb("at_qt", [P, S])
        kt = sb("at_kt", [P, S])
        v_sb = sb("v_sb", [P, T, HD])
        guess = sb("guess", [P, 2, T, R])
        gap = sb("gap", [P, 3, R, S])
        prob = sb("prob", [P, 2, R, S])
        near = sb("near", [P, S])
        junk = sb("junk", [P, S], BF16)
        pt = sb("pt", [P, 2, R * P])
        id_sb = sb("at_id_sb", [P, P])
        idb_words = sb("idb_sb", [P, P // 2], I32)
        idb_sb = idb_words[:].bitcast(BF16)
        cz_words = sb("cz_sb", [P, P // 2], I32)
        cz_sb = cz_words[:].bitcast(BF16)
        bits_sb = sb("bits_sb", [P, 31], I32)
        rank_sb = sb("rank_sb", [P, R, WINDOW])
        floor_sb = sb("floor_sb", [P, 2])
        ones = sb("at_ones", [P, 1])
        part_max = sb("part_max", [P, R, 2])
        row_max = sb("row_max", [P, 2, R])
        thr = sb("thr", [P, 3, R])
        sums = sb("sums", [P, 2, 3, R])
        upd = sb("upd", [P, 5, R])
        miss = sb("miss", [P, 2, R])
        cand = sb("cand", [P, R, PARTS, 8])
        cand2 = sb("cand2", [P, 2, R, PARTS * 8])
        best = sb("best", [P, R, WINDOW])
        hit = sb("hit", [P, R, WINDOW])
        small = sb("small", [P, 6, R])
        cut = sb("cut", [P, 2, R])
        bad = sb("bad", [P, R])
        flag = sb("flag", [1, R + 1], I32)
        f_bits = sb("f_bits", [P, 1], I32)
        f_try = sb("f_try", [P, 1], I32)
        f_mask = sb("f_mask", [P, 1], I32)
        f_count = sb("f_count", [P, 1])
        head_rows = sb("at_head_rows", [R, P])
        den = sb("den", [P, 2, R])
        rden = sb("rden", [P, R])
        dent = sb("dent", [R, P])
        share = sb("share", [P, P])
        ot = sb("ot", [P, 2, P])
        ps_s = pb("at_ps_s", [P, 2, CHUNK])
        ps_t = pb("at_ps_t", [P, 2, 512])
        ps_o = pb("at_ps_o", [P, 512])
        ps_x = pb("at_ps_x", [P, 512])

        consts_in = sem("at_consts_in")
        ones_ready = sem("at_ones_ready")
        qk_in = sem("qk_in")
        v_in = sem("v_in")
        guess_in = sem("guess_in")
        scores_ready = sem("scores_ready")
        scores_read = sem("scores_read")
        max_ready = sem("max_ready")
        gap_ready = sem("gap_ready")
        pool_turns = sem("pool_turns")
        thr_ready = [sem(f"thr_ready{n}") for n in range(3)]
        probed = sem("probed")
        exp_ready = sem("exp_ready")
        kept_ready = sem("kept_ready")
        bad_ready = sem("bad_ready")
        flag_ready = sem("flag_ready")
        flag_read = sem("flag_read")
        pt_turned = sem("pt_turned")
        pt_ready = sem("pt_ready")
        pv_done = sem("pv_done")
        out_ready = sem("out_ready")
        inverse_ready = sem("inverse_ready")
        inverse_turned = sem("inverse_turned")
        dent_ready = sem("dent_ready")
        inverse_spread = sem("inverse_spread")
        share_ready = sem("share_ready")
        ot_stored = [sem("ot_stored0"), sem("ot_stored1")]
        chain = ctx.enter_context(nc.semaphore("at_chain"))
        fchain = ctx.enter_context(nc.semaphore("fchain"))
        prime(nc, primed)
        block = ctx.enter_context(nc.Block("attention"))

        def pieces(s):
            out, n = [], plan.chunk0[s]
            for r in range(R):
                for k0 in range(0, plan.keys[s], CHUNK):
                    out.append((r, k0, min(CHUNK, plan.keys[s] - k0), n))
                    n += 1
            return out

        def block_runs(s):
            n = plan.tile[s] + 1
            return [range(0, n // 8), range(n // 8, 3 * n // 4), range(3 * n // 4, n)]

        @block.sync
        def _(sp):
            for dst, src in ((id_sb, ident), (idb_words, ident_bf), (cz_words, causal_bf), (bits_sb, bits), (rank_sb, ranks),
                             (floor_sb, floors), (head_rows, head_rows_d)):
                sp.dma_start(dst[:], src).then_inc(consts_in, 16)
            with sp.Fori(0, G) as g:
                sp.wait_ge(scores_ready, PRIMED + CH * g)
                sp.dma_start(kt[:], qk_d[g, 0]).then_inc(qk_in, 16)
                sp.dma_start(qt[:], qk_d[g, 1]).then_inc(qk_in, 16)
                sp.wait_ge(thr_ready[2], PRIMED + SE * g)
                sp.dma_start(guess[:], stat_d[g].rearrange("p a (t r) -> p a t r", r=R)).then_inc(guess_in, 16)
                sp.wait_ge(pv_done, PRIMED + BL * g)
                sp.dma_start(v_sb[:], vt_d[:, :, g].rearrange("t p d -> p t d")).then_inc(v_in, 16)

        @block.gpsimd
        def _(pool):
            nc.gpsimd.memset(ones[:], 1.0).then_inc(ones_ready, 1)
            with pool.Fori(0, G) as g:
                for s in range(NB):
                    n = plan.keys[s]
                    pool.wait_ge(max_ready, PRIMED + NB * g + s + 1)
                    pool.sem_inc(pool_turns)
                    for r in range(R):
                        nc.gpsimd.tensor_scalar(gap[:, s % 3, r, 0:n], gap[:, s % 3, r, 0:n], -1.0,
                                                row_max[:, s % 2, r:r + 1], ALU.mult, ALU.add).then_inc(gap_ready, 1)

        @block.tensor
        def _(pe):
            pe.wait_ge(consts_in, PRIMED + 16 * 7)
            pe.wait_ge(ones_ready, PRIMED + 1)
            with pe.Fori(0, G) as g:
                def scores(s, piece):
                    r, k0, n, ch = piece
                    q0 = P * plan.tile[s]
                    rows = slice(HD * r, HD * r + HD)
                    pe.wait_ge(scores_read, PRIMED + CH * g + (ch - 1 if ch >= 2 else 0))
                    for k in range(0, n, 512):
                        w = min(512, n - k)
                        diagonal = k0 + k + w == plan.keys[s]
                        mm = pe.matmul(ps_s[:, ch % 2, k:k + w], qt[rows, q0:q0 + P], kt[rows, k0 + k:k0 + k + w],
                                       start=True, stop=not diagonal, skip_group_check=True)
                        if diagonal:
                            mm = pe.matmul(ps_s[:, ch % 2, k + w - P:k + w], idb_sb, cz_sb,
                                           start=False, stop=True, skip_group_check=True)
                    mm.then_inc(scores_ready, 1)

                def turn_block(s, j):
                    b = plan.block0[s] + j
                    if plan.search[s]:
                        if j == 0:
                            pe.wait_ge(kept_ready, PRIMED + R * SE * g + R * plan.search0[s] + R)
                    elif j == 0:
                        pe.wait_ge(exp_ready, PRIMED + R * NB * g + R * s + R)
                    pe.wait_ge(pt_ready, PRIMED + BL * g + (b - 1 if b >= 2 else 0))
                    for r in range(R):
                        mm = pe.transpose(ps_t[:, b % 2, bass.ts(r, P)], prob[:, s % 2, r, bass.ts(j, P)], id_sb[:])
                    mm.then_inc(pt_turned, 1)

                def times_v(s, j):
                    b = plan.block0[s] + j
                    pe.wait_ge(pt_ready, PRIMED + BL * g + b + 1)
                    if s == 0 and j == 0:
                        pe.wait_ge(v_in, PRIMED + 16 * g + 16)
                    if j == 0:
                        pe.wait_ge(out_ready, PRIMED + NB * g + s)
                    for r in range(R):
                        mm = pe.matmul(ps_o[HD * r:HD * (r + 1), 0:P], v_sb[:, j], pt[:, b % 2, bass.ts(r, P)],
                                       start=(j == 0), stop=(j == plan.tile[s]), skip_group_check=True)
                    mm.then_inc(pv_done, 1)

                def blocks(s, run, between=()):
                    between = list(between)
                    for j in run:
                        turn_block(s, j)
                        take = -(-len(between) // (run.stop - j))
                        for piece in between[:take]:
                            scores(*piece)
                        between = between[take:]
                        if j > run.start:
                            times_v(s, j - 1)
                    if run:
                        times_v(s, run.stop - 1)
                    for piece in between:
                        scores(*piece)

                def turn_inverse(s):
                    pe.wait_ge(inverse_ready, PRIMED + NB * g + s + 1)
                    pe.wait_ge(share_ready, PRIMED + NB * g + s)
                    if s and plan.search[s]:
                        pe.wait_ge(flag_read, PRIMED + SE * g + plan.search0[s] + 1)
                    pe.transpose(ps_x[0:R, P:2 * P], rden[:], id_sb[:]).then_inc(inverse_turned, 1)

                def spread_inverse(s):
                    pe.wait_ge(dent_ready, PRIMED + NB * g + s + 1)
                    pe.matmul(ps_x[:, 2 * P:3 * P], head_rows[:], dent[:], start=True, stop=True).then_inc(inverse_spread, 1)

                def raise_flag(s):
                    n = SE * g + plan.search0[s]
                    pe.wait_ge(bad_ready, PRIMED + n + 1)
                    pe.matmul(ps_x[0:1, 0:R], ones[:], bad[:], start=True, stop=True).then_inc(flag_ready, 1)

                pe.wait_ge(qk_in, PRIMED + 32 * g + 32)
                for piece in pieces(0):
                    scores(0, piece)
                for k in range(NB + 3):
                    ahead = [(k + 1, p) for p in pieces(k + 1)[2 if k else 0:]] if k + 1 < NB else []
                    if 0 <= k - 2 < NB:
                        turn_inverse(k - 2)
                        blocks(k - 2, block_runs(k - 2)[0], ahead[:2])
                        spread_inverse(k - 2)
                        ahead = ahead[2:]
                    for piece in ahead:
                        scores(*piece)
                    if 0 <= k - 2 < NB:
                        blocks(k - 2, block_runs(k - 2)[1])
                    if 0 <= k - 1 < NB and plan.search[k - 1]:
                        if k >= 2:
                            pe.wait_ge(share_ready, PRIMED + NB * g + k - 1)
                        raise_flag(k - 1)
                    for piece in pieces(k + 2)[:2] if k + 2 < NB else []:
                        scores(k + 2, piece)
                    if 0 <= k - 2 < NB:
                        blocks(k - 2, block_runs(k - 2)[2])

        @block.scalar
        def _(act):
            with act.Fori(0, G) as g:
                def copy_block(s, j):
                    b = plan.block0[s] + j
                    act.wait_ge(pt_turned, PRIMED + BL * g + b + 1)
                    act.wait_ge(pv_done, PRIMED + BL * g + (b - 1 if b >= 2 else 0))
                    nc.scalar.activation(pt[:, b % 2], ps_t[:, b % 2], ACT.Copy).then_inc(pt_ready, 1)

                def probe(s, n, r):
                    m = SE * g + plan.search0[s]
                    if r == 0:
                        act.wait_ge(thr_ready[n], PRIMED + m + 1)
                    if n == 0:
                        act.wait_ge(gap_ready, PRIMED + R * NB * g + R * s + r + 1)
                    N = plan.keys[s]
                    act.wait_ge(probed, PRIMED + 3 * R * m + R * n + r)
                    nc.scalar.activation(junk[:, 0:N], gap[:, s % 3, r, 0:N], ACT.Sign, bias=thr[:, s % 3, r:r + 1], scale=-1.0,
                                         accum_out=sums[:, s % 2, n, r:r + 1]).then_inc(probed, 1)

                def weights(s, r):
                    N = plan.keys[s]
                    if not plan.search[s]:
                        act.wait_ge(gap_ready, PRIMED + R * NB * g + R * s + r + 1)
                    sums_too = {} if plan.search[s] else {"accum_out": den[:, s % 2, r:r + 1]}
                    nc.scalar.activation(prob[:, s % 2, r, 0:N], gap[:, s % 3, r, 0:N], ACT.Exp, scale=-1.0, **sums_too).then_inc(exp_ready, 1)

                def copy_inverse(s):
                    act.wait_ge(inverse_turned, PRIMED + NB * g + s + 1)
                    nc.scalar.activation(dent[:], ps_x[0:R, P:2 * P], ACT.Copy).then_inc(dent_ready, 1)

                def copy_share(s):
                    act.wait_ge(inverse_spread, PRIMED + NB * g + s + 1)
                    act.wait_ge(out_ready, PRIMED + NB * g + s)
                    nc.scalar.activation(share[:], ps_x[:, 2 * P:3 * P], ACT.Copy).then_inc(share_ready, 1)

                def store(s):
                    act.wait_ge(out_ready, PRIMED + NB * g + s + 1)
                    act.dma_start(at_d[plan.tile[s], :, g], ot[:, s % 2]).then_inc(ot_stored[s % 2], 16)

                for k in range(NB + 3):
                    runs = block_runs(k - 2) if 0 <= k - 2 < NB else [(), (), ()]
                    here = 0 <= k < NB and plan.search[k]
                    probes = [[lambda r=r, n=n: probe(k, n, r) for r in range(R)] if here else [] for n in range(3)]
                    if 0 <= k - 1 < NB:
                        probes[0] += [lambda r=r: weights(k - 1, r) for r in range(R)]
                    if 0 <= k - 2 < NB:
                        copy_inverse(k - 2)
                    for n in range(3):
                        left = list(runs[n])
                        for m, item in enumerate(probes[n]):
                            item()
                            take = -(-len(left) // (len(probes[n]) - m))
                            for j in left[:take]:
                                copy_block(k - 2, j)
                            left = left[take:]
                        for j in left:
                            copy_block(k - 2, j)
                        if n == 0 and 0 <= k - 2 < NB:
                            copy_share(k - 2)
                        if n == 0 and k - 4 >= 0:
                            store(k - 4)
                store(NB - 1)
            for h in range(2):
                act.wait_ge(ot_stored[h], PRIMED + 16 * G * NB // 2)

        @block.vector
        def _(dve):
            V = nc.vector
            dve.wait_ge(consts_in, PRIMED + 16 * 7)
            with dve.Fori(0, G) as g:
                dve.sem_clear(chain)
                put, sync = paced(dve, chain)

                def step(instruction):
                    put(instruction)
                    sync()

                def read_scores(s, piece):
                    r, k0, n, ch = piece
                    dve.wait_ge(scores_ready, PRIMED + CH * g + ch + 1)
                    V.tensor_scalar(gap[:, s % 3, r, k0:k0 + n], ps_s[:, ch % 2, 0:n], SCALE, None, ALU.mult, ALU.max,
                                    accum_out=part_max[:, r, k0 // CHUNK:k0 // CHUNK + 1]).then_inc(scores_read, 1)

                def first_guess(s):
                    dve.wait_ge(scores_read, PRIMED + CH * g + plan.chunk0[s + 1])
                    if plan.chunks[s] > R:
                        last = V.tensor_reduce(row_max[:, s % 2], part_max[:], AX, ALU.max)
                    else:
                        last = V.tensor_copy(row_max[:, s % 2], part_max[:, :, 0])
                    last.then_inc(max_ready, 1)
                    dve.wait_ge(max_ready, PRIMED + NB * g + s + 1)
                    if plan.search[s]:
                        V.tensor_tensor(thr[:, s % 3], row_max[:, s % 2], guess[:, 0, plan.tile[s]], ALU.subtract).then_inc(thr_ready[0], 1)

                def better_guess(s, n):
                    m = SE * g + plan.search0[s]
                    dve.wait_ge(probed, PRIMED + 3 * R * m + R * n)
                    first, off = miss[:, 0], miss[:, n - 1]
                    step(V.tensor_scalar(off, sums[:, s % 2, n - 1], -0.5, AIM - plan.keys[s] / 2, ALU.mult, ALU.add))
                    step(V.tensor_tensor(upd[:, 1], off, guess[:, 1, plan.tile[s]], ALU.mult))
                    if n == 2:
                        V.tensor_tensor(upd[:, 2], off, off, ALU.mult)
                        V.tensor_tensor(upd[:, 3], first, first, ALU.mult)
                        step(V.tensor_tensor(upd[:, 4], first, off, ALU.mult))
                        step(V.scalar_tensor_tensor(upd[:, 4], upd[:, 4], -0.01, upd[:, 3], ALU.min, ALU.subtract))
                        step(V.reciprocal(upd[:, 0], upd[:, 4]))
                        step(V.scalar_tensor_tensor(upd[:, 3], upd[:, 3], -1.0, upd[:, 0], ALU.mult, ALU.mult))
                        step(V.scalar_tensor_tensor(upd[:, 1], upd[:, 2], NEAR * NEAR, upd[:, 1], ALU.is_gt, ALU.mult))
                        step(V.tensor_tensor(upd[:, 1], upd[:, 1], upd[:, 3], ALU.mult))
                    V.tensor_tensor(thr[:, s % 3], thr[:, s % 3], upd[:, 1], ALU.add).then_inc(thr_ready[n], 1)

                def candidates(s, r, between):
                    N = plan.keys[s]
                    w = gap[:, s % 3, r, 0:N]
                    if r == 0:
                        dve.wait_ge(thr_ready[2], PRIMED + SE * g + plan.search0[s] + 1)
                    sync()
                    put(V.scalar_tensor_tensor(near[:, 0:N], w, thr[:, s % 3, r:r + 1], w, ALU.is_le, ALU.mult))
                    between()
                    sync()
                    for p in range(PARTS):
                        last = V.max(cand[:, r, p], near[:, p * N // PARTS:(p + 1) * N // PARTS])
                    put(last)
                    between()

                def rounds():
                    sync()
                    pool = [cand[:, r].rearrange("p a b -> p (a b)") for r in range(R)]
                    for n in range(ROUNDS):
                        for r in range(R):
                            last = V.max(best[:, r, 8 * n:8 * n + 8], pool[r])
                        step(last)
                        if n < ROUNDS - 1:
                            for r in range(R):
                                last = V.match_replace(cand2[:, n, r], best[:, r, 8 * n:8 * n + 8], pool[r], -1.0)
                                pool[r] = cand2[:, n, r]
                            step(last)

                def settle(s):
                    m = SE * g + plan.search0[s]
                    c = cut[:, s % 2]
                    t = thr[:, s % 3]
                    wide = lambda ap: spread(ap.unsqueeze(2), [P, R, WINDOW])
                    step(V.tensor_tensor(hit[:], best[:], wide(t), ALU.is_equal))
                    step(V.tensor_reduce(small[:, 0], hit[:], AX, ALU.add))
                    dve.wait_ge(probed, PRIMED + 3 * R * m + 3 * R)
                    step(V.tensor_tensor(small[:, 1], small[:, 0], sums[:, s % 2, 2], ALU.add))
                    step(V.tensor_scalar(small[:, 0], small[:, 1], 0.5, plan.keys[s] / 2 - KEEP, ALU.mult, ALU.add))
                    step(V.tensor_tensor(hit[:], rank_sb[:], wide(small[:, 0]), ALU.is_equal))
                    step(V.tensor_tensor(hit[:], hit[:], best[:], ALU.mult))
                    V.tensor_scalar(small[:, 2], small[:, 0], -(WINDOW - 1) / 2, None, ALU.add)
                    step(V.tensor_reduce(c, hit[:], AX, ALU.add))
                    V.tensor_tensor(small[:, 5], small[:, 2], small[:, 2], ALU.mult)
                    step(V.tensor_reduce(small[:, 1], cand[:, :, :, 7], AX, ALU.max))
                    V.tensor_tensor(small[:, 3], small[:, 1], c, ALU.is_gt)
                    step(V.tensor_tensor(small[:, 4], small[:, 1], t, ALU.is_ge))
                    step(V.tensor_tensor(small[:, 3], small[:, 3], small[:, 4], ALU.max))
                    last = V.scalar_tensor_tensor(bad[:], small[:, 5], (WINDOW / 2) ** 2, small[:, 3], ALU.is_gt, ALU.max)
                    if plan.tile[s] == 1:
                        step(last)
                        step(V.tensor_scalar(c, c, floor_sb[:, 0:1], None, ALU.max))
                        last = V.tensor_scalar(bad[:], bad[:], floor_sb[:, 1:2], None, ALU.mult)
                    last.then_inc(bad_ready, 1)

                def check_flag(s):
                    m = SE * g + plan.search0[s]
                    dve.wait_ge(flag_ready, PRIMED + m + 1)
                    V.tensor_copy(flag[:, 0:R], ps_x[0:1, 0:R]).then_inc(flag_read, 1)
                    dve.wait_ge(flag_read, PRIMED + m + 1)
                    step(V.tensor_reduce(flag[:, R:R + 1], flag[:, 0:R], AX, ALU.max))
                    found = dve.value_load(flag[0:1, R:R + 1])
                    with dve.If(found > 0):
                        for r in range(R):
                            one = dve.value_load(flag[0:1, r:r + 1])
                            with dve.If(one > 0):
                                bisect(s, r)
                        dve.sem_clear(fchain)

                def bisect(s, r):
                    N = plan.keys[s]
                    dve.sem_clear(fchain)
                    fstep = ordered(dve, fchain)
                    fstep(V.memset(f_bits[:], 0))
                    with dve.Fori(0, 31) as i:
                        dve.sem_clear(fchain)
                        fstep = ordered(dve, fchain)
                        bit = bits_sb[:, bass.ds(i, 1)]
                        fstep(V.tensor_tensor(f_try[:], f_bits[:], bit, ALU.bitwise_or))
                        fstep(V.tensor_scalar(near[:, 0:N], gap[:, s % 3, r, 0:N], f_try[:].bitcast(F32), None,
                                              ALU.is_lt, ALU.add, accum_out=f_count[:]))
                        fstep(V.tensor_scalar(f_mask[:], f_count[:], KEEP - 0.5, -1.0, ALU.is_lt, ALU.mult))
                        fstep(V.tensor_tensor(f_mask[:], f_mask[:], bit, ALU.bitwise_and))
                        fstep(V.tensor_tensor(f_bits[:], f_bits[:], f_mask[:], ALU.bitwise_or))
                    dve.sem_clear(fchain)
                    fstep = ordered(dve, fchain)
                    c = cut[:, s % 2, r:r + 1]
                    fstep(V.tensor_copy(c, f_bits[:].bitcast(F32)))
                    if plan.tile[s] == 1:
                        fstep(V.tensor_scalar(c, c, floor_sb[:, 0:1], None, ALU.max))

                def keep(s, r):
                    N = plan.keys[s]
                    dve.wait_ge(exp_ready, PRIMED + R * NB * g + R * s + r + 1)
                    V.scalar_tensor_tensor(prob[:, s % 2, r, 0:N], gap[:, s % 3, r, 0:N], cut[:, s % 2, r:r + 1],
                                           prob[:, s % 2, r, 0:N], ALU.is_le, ALU.mult,
                                           accum_out=den[:, s % 2, r:r + 1]).then_inc(kept_ready, 1)

                def invert(s):
                    if plan.search[s]:
                        dve.wait_ge(kept_ready, PRIMED + R * SE * g + R * plan.search0[s] + R)
                    else:
                        dve.wait_ge(exp_ready, PRIMED + R * NB * g + R * s + R)
                    dve.wait_ge(inverse_turned, PRIMED + NB * g + s)
                    V.reciprocal(rden[:], den[:, s % 2]).then_inc(inverse_ready, 1)

                def normalize(s):
                    dve.wait_ge(pv_done, PRIMED + BL * g + plan.block0[s + 1])
                    dve.wait_ge(share_ready, PRIMED + NB * g + s + 1)
                    dve.wait_ge(ot_stored[s % 2], PRIMED + (NB // 2) * 16 * g + 16 * (s // 2))
                    V.tensor_tensor(ot[:, s % 2], ps_o[:, 0:P], share[:], ALU.mult).then_inc(out_ready, 1)

                dve.wait_ge(guess_in, PRIMED + 16 * g + 16)
                for piece in pieces(0):
                    read_scores(0, piece)
                first_guess(0)
                for k in range(NB + 3):
                    mine = 0 <= k - 1 < NB and plan.search[k - 1]
                    here = 0 <= k < NB and plan.search[k]
                    ahead = pieces(k + 1) if k + 1 < NB else []

                    def some(n):
                        for piece in ahead[:n]:
                            read_scores(k + 1, piece)
                        del ahead[:n]

                    if mine:
                        old = [k - 3] if k >= 3 else []

                        def between():
                            some(1)
                            if old:
                                normalize(old.pop())

                        for r in range(R):
                            candidates(k - 1, r, between)
                            if r == 2 and here:
                                better_guess(k, 1)
                        some(8)
                        if k + 1 < NB:
                            first_guess(k + 1)
                        rounds()
                    else:
                        if 0 <= k - 3 < NB:
                            normalize(k - 3)
                        some(8)
                        if here:
                            better_guess(k, 1)
                        if k + 1 < NB:
                            first_guess(k + 1)
                    if mine:
                        settle(k - 1)
                    if here:
                        better_guess(k, 2)
                    if mine:
                        check_flag(k - 1)
                        for r in range(R):
                            keep(k - 1, r)
                    if 0 <= k - 1 < NB:
                        invert(k - 1)


def output_program(nc, x, wo, wf, bb, at_d, xt_d, zp_d, out):
    with ExitStack() as ctx:
        sb = lambda n, s, d=F32: ctx.enter_context(nc.sbuf_tensor(n, s, d))
        primed = []
        sem = semaphores(nc, ctx, primed)
        wo_sb = sb("wo_sb", [P, C, D])
        wf_sb = sb("wf_sb", [P, C, D])
        bb_sb = sb("bb_sb", [RANK + 1, D])
        at = sb("o_at", [P, 2, C, P])
        xt = sb("o_xt", [P, 2, C, P])
        zp = sb("o_zp", [RANK + 1, 2, P])
        xr = sb("o_xr", [P, 2, D])
        y = sb("o_y", [P, 2, D])
        ps = ctx.enter_context(nc.psum_tensor("o_ps", [P, 2, D], F32))
        weights_in = [sem(f"o_weights_in{n}") for n in range(4)]
        tile_in = [sem("o_tile_in0"), sem("o_tile_in1")]
        summed = sem("o_summed")
        done = sem("o_done")
        stored = [sem("o_stored0"), sem("o_stored1")]
        prime(nc, primed)
        block = ctx.enter_context(nc.Block("output"))

        @block.sync
        def _(sp):
            def load(i, h):
                t = 2 * i + h
                sp.wait_ge(done, PRIMED + two_before(i, h))
                sp.dma_start(xt[:, h], xt_d[t]).then_inc(tile_in[h], 16)
                sp.dma_start(at[:, h], at_d[t]).then_inc(tile_in[h], 16)
                sp.dma_start(zp[:, h], zp_d[:, bass.ts(t, P)]).then_inc(tile_in[h], 16)
                sp.dma_start(xr[:, h], x[t]).then_inc(tile_in[h], 16)

            for h in range(2):
                load(0, h)
            with sp.Fori(1, T // 2) as i:
                for h in range(2):
                    load(i, h)

        @block.scalar
        def _(act):
            act.dma_start(wf_sb[:, :, 0:512], wf[:, :, 0:512]).then_inc(weights_in[0], 16)
            act.wait_ge(weights_in[0], PRIMED + 16)
            act.dma_start(wo_sb[:], wo).then_inc(weights_in[3], 16)
            act.dma_start(bb_sb[:], bb).then_inc(weights_in[2], 16)
            act.dma_start(wf_sb[:, :, 512:D], wf[:, :, 512:D]).then_inc(weights_in[1], 16)
            with act.Fori(0, T // 2) as i:
                for h in range(2):
                    act.wait_ge(done, PRIMED + 2 * i + h + 1)
                    act.dma_start(out[2 * i + h], y[:, h]).then_inc(stored[h], 16)
            for h in range(2):
                act.wait_ge(stored[h], PRIMED + 16 * (T // 2))

        @block.tensor
        def _(pe):
            def products(i, h):
                pe.wait_ge(tile_in[h], PRIMED + 64 * i + 64)
                pe.wait_ge(done, PRIMED + two_before(i, h))
                for j in range(2):
                    cols = bass.ts(j, 512)
                    pe.wait_ge(weights_in[j], PRIMED + 16)
                    for c in range(C):
                        pe.matmul(ps[:, h, cols], xt[:, h, c], wf_sb[:, c, cols], start=(c == 0), stop=False)
                    pe.wait_ge(weights_in[3], PRIMED + 16)
                    for c in range(C):
                        pe.matmul(ps[:, h, cols], at[:, h, c], wo_sb[:, c, cols], start=False, stop=False)
                    pe.wait_ge(weights_in[2], PRIMED + 16)
                    mm = pe.matmul(ps[:, h, cols], zp[:, h], bb_sb[:, cols], start=False, stop=True)
                mm.then_inc(summed, 1)

            for h in range(2):
                products(0, h)
            with pe.Fori(1, T // 2) as i:
                for h in range(2):
                    products(i, h)

        @block.vector
        def _(dve):
            with dve.Fori(0, T // 2) as i:
                for h in range(2):
                    dve.wait_ge(summed, PRIMED + 2 * i + h + 1)
                    dve.wait_ge(stored[h], PRIMED + 16 * i)
                    nc.vector.tensor_tensor(y[:, h], ps[:, h], xr[:, h], ALU.add).then_inc(done, 1)


def build(nc, a):
    with ExitStack() as ctx:
        dram = lambda n, s: nc.dram_tensor(n, s, F32).ap()
        xt_d = dram("xt_d", [T, P, C, P])
        vt_d = dram("vt_d", [T, P, G, HD])
        zp_d = dram("zp_d", [RANK + 1, S])
        qk_d = dram("qk_d", [G, 2, P, S])
        stat_d = dram("stat_d", [G, P, 2, T * R])
        at_d = dram("at_d", [T, P, G, P])
        x = a["x"].rearrange("(t p) d -> t p d", p=P)
        with ExitStack() as early:
            z_keep = early.enter_context(nc.sbuf_tensor("z_keep", [RANK, S], F32))
            gate_in = early.enter_context(nc.sbuf_tensor("gate_in", [A, T, 2 * E], F32))
            tokens_program(nc, x, a["wv"], a["a_in"], a["w8"], a["b8"], a["lime_t"], a["ident"], xt_d, vt_d, z_keep, gate_in)
            router_program(nc, a["lime"], a["ident"], zp_d, z_keep, gate_in)
        heads_program(nc, a["wqk"], xt_d, a["cos"], a["sin"], a["rot_t"], a["repeat"], a["ident"], a["block_mean"], a["head_sel"], a["zrow"], qk_d, stat_d)
        attention_program(nc, qk_d, vt_d, stat_d, at_d, a["ident"], a["ident_bf"], a["causal_bf"], a["bits"], a["ranks"], a["floors"], a["head_rows"])
        output_program(nc, x, a["wo"], a["wf"], a["bb"], at_d, xt_d, zp_d, a["out"].rearrange("(t p) d -> t p d", p=P))


def normal_tail(share):
    low, high = -10.0, 10.0
    for _ in range(60):
        z = (low + high) / 2
        if math.erfc(z / math.sqrt(2)) / 2 > share:
            low = z
        else:
            high = z
    return z


def as_bf16(table):
    upper = (np.ascontiguousarray(table, np.float32).view(np.uint32) >> 16).astype(np.uint16)
    return upper.view(np.int32)


def constants():
    f = np.float32
    inv = f(1) / np.power(f(10000), np.arange(0, HD, 2, dtype=f) / f(HD))
    angle = np.arange(S, dtype=f)[:, None] * inv
    lay = lambda t: np.ascontiguousarray(np.tile(np.concatenate([t, t], 1).T, (R, 1)))
    rot = np.zeros((P, P), f)
    for h in range(R):
        for d in range(HD // 2):
            rot[HD * h + d, HD * h + d + HD // 2] = -1
            rot[HD * h + d + HD // 2, HD * h + d] = 1
    same = np.kron(np.eye(R), np.ones((HD, HD)))
    zrow = np.zeros((3, S))
    for n in range(1, S + 1):
        if n < KEEP + WINDOW:
            zrow[1, n - 1] = -BIG
        else:
            z = normal_tail(AIM / n)
            zrow[0, n - 1] = z
            zrow[2, n - 1] = math.sqrt(2 * math.pi) * math.exp(z * z / 2) / n
    zrow = np.repeat(zrow.reshape(3, T, P).transpose(2, 0, 1)[..., None], R, -1).reshape(P, 3, T * R)
    row = np.arange(P)
    few = P + row + 1 < KEEP
    return {
        "ident": np.eye(P, dtype=f), "rot_t": np.ascontiguousarray(rot.T),
        "cos": lay(np.cos(angle)), "sin": lay(np.sin(angle)),
        "repeat": np.tile(np.eye(HD, dtype=f), (R, R)),
        "block_mean": (same * (SCALE * SCALE / S)).astype(f),
        "head_sel": np.kron(np.eye(R), np.ones((HD, 1))).astype(f),
        "head_rows": np.kron(np.eye(R), np.ones((1, HD))).astype(f),
        "zrow": zrow.astype(f),
        "ident_bf": as_bf16(np.eye(P)),
        "causal_bf": as_bf16(np.where(row[:, None] < row[None, :], MASKED, 0)),
        "bits": np.tile((1 << np.arange(30, -1, -1)).astype(np.int32), (P, 1)),
        "ranks": np.tile(np.arange(WINDOW, dtype=f), (P, R, 1)),
        "floors": np.stack([np.where(few, BIG, 0), np.where(few, 0, 1)], 1).astype(f),
    }


def kernel(**inputs):
    import concourse.bacc as bacc
    from concourse.bass_utils import run_bass_kernel_spmd

    n = {k: np.asarray(v) for k, v in inputs.items()}
    by_chunk = lambda w: np.ascontiguousarray(w.T.reshape(C, P, -1).transpose(1, 0, 2))
    wq = by_chunk(n["L0_attn_Wq"]).reshape(P, C, G, P)
    wk = by_chunk(n["L0_attn_Wk"]).reshape(P, C, G, 1, HD)
    wk = np.broadcast_to(wk, (P, C, G, R, HD)).reshape(P, C, G, P)
    arrays = {
        "x": n["L0_attn_hidden_states"].reshape(S, D),
        "wqk": np.ascontiguousarray(np.concatenate([wk, wq], -1).transpose(2, 0, 1, 3)),
        "wv": by_chunk(n["L0_attn_Wv"]),
        "wo": by_chunk(n["L0_attn_Wo"]),
        "wf": by_chunk(n["L0_ffn_W"]),
        "w8": by_chunk(n["L0_ffn_W"][:E]),
        "b8": np.ascontiguousarray(n["L0_ffn_b"][None, :E]),
        "a_in": np.ascontiguousarray(n["L0_ffn_A"].reshape(C, P, RANK).transpose(1, 0, 2)),
        "bb": np.concatenate([n["L0_ffn_Bmat"], n["L0_ffn_b"][None]], 0),
        "lime": n["L0_ffn_LiMEs"],
        "lime_t": np.ascontiguousarray(n["L0_ffn_LiMEs"].T),
        **constants(),
    }
    arrays = {k: np.ascontiguousarray(v) for k, v in arrays.items()}
    nc = bacc.Bacc("TRN2", target_bir_lowering=False, num_devices=1)
    aps = {k: nc.dram_tensor(k, v.shape, mybir.dt.from_np(v.dtype), kind="ExternalInput").ap() for k, v in arrays.items()}
    aps["out"] = nc.dram_tensor("out", (S, D), F32, kind="ExternalOutput").ap()
    build(nc, aps)
    r = run_bass_kernel_spmd(nc, [arrays], core_ids=[0])
    return r.results[0]["out"].reshape(1, S, D)
```
